# Optimizing a Trainium2 kernel written in Bass

```python
import numpy as np
import jax
import jax.numpy as jnp

def _softmax(x, axis=-1):
    return jax.nn.softmax(x, axis=axis)

def _gelu(x):
    return jax.nn.gelu(x, approximate=True)

def _silu(x):
    return jax.nn.silu(x)

def _sigmoid(x):
    return jax.nn.sigmoid(x)

def _layernorm(x, axis=-1, eps=1e-05):
    m = jnp.mean(x, axis=axis, keepdims=True)
    v = jnp.var(x, axis=axis, keepdims=True)
    return (x - m) / jnp.sqrt(v + eps)

def _scatter_add(tgt, idx, src, axis=0):
    return tgt.at[idx].add(src)

def _segment_sum(src, seg, n):
    return jax.ops.segment_sum(src, seg, n)
kernel_name = 'mk_xattn_ffn_d1_seqx_r8_f92dd9'

def setup_inputs(seed: int=0):
    np.random.seed(seed)
    _w = jnp.asarray

    def _rec_inputs():
        import jax
        import jax.numpy as jnp
        _rk = jax.random.key(seed)
        x = -0.0002928 + 1 * jax.random.normal(jax.random.fold_in(_rk, 1), (64, 64, 128), jnp.float32)
        _lenS = 64 - jax.random.randint(jax.random.fold_in(_rk, 7), (64,), 0, max(1, 64 // 4) + 1, jnp.int32)
        _lenS2 = 64 - jax.random.randint(jax.random.fold_in(_rk, 8), (64,), 0, max(1, 64 // 4) + 1, jnp.int32)
        _ctx_1024P = jax.random.normal(jax.random.fold_in(_rk, 11), (64, 16, 128), jnp.float32)
        _ctx_1024c = jax.random.dirichlet(jax.random.fold_in(_rk, 511), 0.3 * jnp.ones((16,), jnp.float32), (64, 64))
        _ctx_1024t = jnp.einsum('bsk,bkd->bsd', _ctx_1024c, _ctx_1024P)
        _ctx_1024t = _ctx_1024t * jax.lax.rsqrt(jnp.mean(jnp.square(_ctx_1024t)) + 1e-12) * 0.953939
        ctx_1024 = -1.39393e-06 + 0.999914 * (_ctx_1024t + 0.3 * jax.random.normal(jax.random.fold_in(_rk, 611), (64, 64, 128), jnp.float32))
        return (x, ctx_1024)
    x, ctx_1024 = _rec_inputs()

    def _L0_xattn_setup():
        import jax, jax.numpy as jnp
        import numpy as np
        D_MODEL = 128
        NUM_HEADS = 16
        D_K = D_MODEL // NUM_HEADS
        key = jax.random.key(seed)
        ks = jax.random.split(key, 11)
        B, S = (2, 256)
        s = 1.0 / np.sqrt(D_MODEL)
        inp = {'q': jax.random.normal(ks[0], (B, S, D_MODEL), jnp.float32), 'k': jax.random.normal(ks[1], (B, S, D_MODEL), jnp.float32), 'v': jax.random.normal(ks[2], (B, S, D_MODEL), jnp.float32), 'Wq': jax.random.normal(ks[3], (D_MODEL, D_MODEL), jnp.float32) * s, 'bq': jax.random.normal(ks[4], (D_MODEL,), jnp.float32) * 0.01, 'Wk': jax.random.normal(ks[5], (D_MODEL, D_MODEL), jnp.float32) * s, 'bk': jax.random.normal(ks[6], (D_MODEL,), jnp.float32) * 0.01, 'Wv': jax.random.normal(ks[7], (D_MODEL, D_MODEL), jnp.float32) * s, 'bv': jax.random.normal(ks[8], (D_MODEL,), jnp.float32) * 0.01, 'Wo': jax.random.normal(ks[9], (D_MODEL, D_MODEL), jnp.float32) * s, 'bo': jax.random.normal(ks[10], (D_MODEL,), jnp.float32) * 0.01}
        return inp
    _L0_xattn_all = _L0_xattn_setup()
    _L0_xattn_in = {k: v for k, v in _L0_xattn_all.items() if k in ('Wq', 'bq', 'Wk', 'bk', 'Wv', 'bv', 'Wo', 'bo')}
    del _L0_xattn_all

    def _L0_ffn_setup():
        import jax, jax.numpy as jnp
        import numpy as np
        HIDDEN = 128
        NUM_EXPERTS = 8
        CAPACITY_FACTOR = 1.25
        key = jax.random.key(seed)
        k_tok, k_g, k_w1, k_b1, k_w2, k_b2 = jax.random.split(key, 6)
        B, S, H, E = (4, 256, HIDDEN, NUM_EXPERTS)
        tokens = jax.random.normal(k_tok, (B, S, H), dtype=jnp.float32)
        gate_w = jax.random.normal(k_g, (E, H), dtype=jnp.float32) * 0.02
        W1 = jax.random.normal(k_w1, (E, H, H), dtype=jnp.float32) * 0.02
        b1 = jax.random.normal(k_b1, (E, H), dtype=jnp.float32) * 0.02
        W2 = jax.random.normal(k_w2, (E, H, H), dtype=jnp.float32) * 0.02
        b2 = jax.random.normal(k_b2, (E, H), dtype=jnp.float32) * 0.02
        return {'tokens': tokens, 'gate_w': gate_w, 'W1': W1, 'b1': b1, 'W2': W2, 'b2': b2}
    _L0_ffn_all = _L0_ffn_setup()
    _L0_ffn_in = {k: v for k, v in _L0_ffn_all.items() if k in ('gate_w', 'W1', 'b1', 'W2', 'b2')}
    del _L0_ffn_all
    return {'x': x, 'ctx_1024': ctx_1024, 'L0_xattn_Wq': _L0_xattn_in['Wq'], 'L0_xattn_bq': _L0_xattn_in['bq'], 'L0_xattn_Wk': _L0_xattn_in['Wk'], 'L0_xattn_bk': _L0_xattn_in['bk'], 'L0_xattn_Wv': _L0_xattn_in['Wv'], 'L0_xattn_bv': _L0_xattn_in['bv'], 'L0_xattn_Wo': _L0_xattn_in['Wo'], 'L0_xattn_bo': _L0_xattn_in['bo'], 'L0_ffn_gate_w': _L0_ffn_in['gate_w'], 'L0_ffn_W1': _L0_ffn_in['W1'], 'L0_ffn_b1': _L0_ffn_in['b1'], 'L0_ffn_W2': _L0_ffn_in['W2'], 'L0_ffn_b2': _L0_ffn_in['b2']}

def reference(x, ctx_1024, L0_xattn_Wq, L0_xattn_bq, L0_xattn_Wk, L0_xattn_bk, L0_xattn_Wv, L0_xattn_bv, L0_xattn_Wo, L0_xattn_bo, L0_ffn_gate_w, L0_ffn_W1, L0_ffn_b1, L0_ffn_W2, L0_ffn_b2):
    import jax
    import jax.numpy as jnp

    def _L0_xattn_ref(q, k, v, Wq, bq, Wk, bk, Wv, bv, Wo, bo):
        import jax, jax.numpy as jnp
        import numpy as np
        D_MODEL = 128
        NUM_HEADS = 16
        D_K = D_MODEL // NUM_HEADS
        B, S, _ = q.shape

        def heads(x, W, b):
            y = x @ W.T + b
            return y.reshape(B, -1, NUM_HEADS, D_K).transpose(0, 2, 1, 3)
        qh = heads(q, Wq, bq)
        kh = heads(k, Wk, bk)
        vh = heads(v, Wv, bv)
        scores = jnp.einsum('bhqd,bhkd->bhqk', qh, kh) / jnp.sqrt(jnp.float32(D_K))
        attn = jax.nn.softmax(scores, axis=-1)
        out = jnp.einsum('bhqk,bhkd->bhqd', attn, vh)
        out = out.transpose(0, 2, 1, 3).reshape(B, S, D_MODEL)
        return out @ Wo.T + bo

    def _L0_ffn_ref(tokens, gate_w, W1, b1, W2, b2):
        import jax, jax.numpy as jnp
        import numpy as np
        HIDDEN = 128
        NUM_EXPERTS = 8
        CAPACITY_FACTOR = 1.25
        B, S, H = tokens.shape
        E = gate_w.shape[0]
        T = B * S
        x = tokens.reshape(T, H)
        logits = x @ gate_w.T
        probs = jax.nn.softmax(logits, axis=-1)
        top2_w, top2_idx = jax.lax.top_k(probs, 2)
        cap = int(CAPACITY_FACTOR * T / E)
        counts = jnp.bincount(top2_idx.reshape(-1), length=E)
        keep = (counts <= cap).astype(x.dtype)
        comb = jnp.zeros((T, E), dtype=x.dtype).at[jnp.arange(T)[:, None], top2_idx].add(top2_w)
        comb = comb * keep[None, :]
        h = jax.nn.relu(jnp.einsum('th,ehf->tef', x, W1) + b1[None, :, :])
        y = jnp.einsum('teh,ehf->tef', h, W2) + b2[None, :, :]
        out = jnp.einsum('te,tef->tf', comb, y)
        return out.reshape(B, S, H)
    x = x + _L0_xattn_ref(_layernorm(x, axis=-1), ctx_1024, ctx_1024, L0_xattn_Wq, L0_xattn_bq, L0_xattn_Wk, L0_xattn_bk, L0_xattn_Wv, L0_xattn_bv, L0_xattn_Wo, L0_xattn_bo)
    x = x + _L0_ffn_ref(_layernorm(x, axis=-1), L0_ffn_gate_w, L0_ffn_W1, L0_ffn_b1, L0_ffn_W2, L0_ffn_b2)
    return x

_drawn_inputs = setup_inputs


def setup_inputs(seed=0):
    import zlib

    import numpy as np

    out = dict(_drawn_inputs(seed))
    spreads = {}
    factors = {'L0_xattn_bq': 25.69, 'L0_xattn_bk': 64.0, 'L0_xattn_bv': 5.706, 'L0_xattn_bo': 5.725}
    for name, (base, spread) in spreads.items():
        noise = np.random.default_rng([zlib.crc32(name.encode()), seed]).standard_normal(out[name].shape)
        drawn = base * np.exp(spread * noise) if base else spread * noise
        out[name] = jnp.asarray(drawn.astype(out[name].dtype))
    for name, factor in factors.items():
        out[name] = (out[name] * factor).astype(out[name].dtype)
    return out
```

```python
from contextlib import ExitStack

import concourse.bass as bass
from concourse import mybir

F32 = mybir.dt.float32
BF16 = mybir.dt.bfloat16
I32 = mybir.dt.int32
ALU = mybir.AluOpType
ACT = mybir.ActivationFunctionType
AX = mybir.AxisListType

B, S, D = 64, 64, 128
H, DK = 16, 8
E = 8
TOK = B * S
P = 128
GT = 512
GB = GT // S
G = TOK // GT
NT = GT // P
PAIRS = H // 2
CAP = int(1.25 * TOK / E)
EPS = 1e-5
SCALE = DK ** -0.5
PARTS = 3
PRODUCTS = [(0, 0), (0, 1), (1, 0), (1, 1), (0, 2), (2, 0)]
ROWS = len(PRODUCTS) * 2 * DK
SHIFT_ROWS = 2 * PARTS
DX = D + E
ORDER = [0, 2, 4, 6, 1, 3, 5, 7]
HALF = PAIRS // 2
SPREADS = 16 * len(PRODUCTS)
W_Q, W_K, W_V, W_OT, W_ON = 0, D, 2 * D, 3 * D, 3 * D + DX
W_G = W_ON + D
W_BIAS = W_G + E
W_COLS = W_BIAS + 4
C_IDENT, C_CENTRE, C_ONES = 0, DX, DX + D
C_DESC = C_ONES + 64
C_MASK = C_DESC + NT * E
C_COLS = C_MASK + 2


class Chain:

    def __init__(self, eng, sem, base):
        self.eng, self.sem, self.base, self.n = eng, sem, base, 0

    def link(self, ins):
        ins.then_inc(self.sem, 1)
        self.n += 1
        self.eng.wait_ge(self.sem, self.base + self.n)


def build(nc, x_nat, x_t, ctx_t, weights, consts, shift_ones, ident_b, w1, w2, b1_t, b2_rows, out):
    ctx = ExitStack()
    with ctx:
        def sb(name, shape, dt=F32):
            return ctx.enter_context(nc.sbuf_tensor(name, shape, dt))

        def ps(name):
            return ctx.enter_context(nc.psum_tensor(name, [P, 512], F32))

        def sem(name):
            return ctx.enter_context(nc.semaphore(name))

        wts = sb("wts", [P, W_COLS])
        cst = sb("cst", [P, C_COLS])
        identb = sb("identb", [P, P], BF16)
        onesb = sb("onesb", [P, P], BF16)
        bv_wide = sb("bv_wide", [P, P])
        bo_wide = sb("bo_wide", [P, P])
        bias_row = sb("bias_row", [P, DX])
        xin = [sb(f"xin{i}", [P, NT, D]) for i in range(2)]
        ctxT = [sb(f"ctxT{i}", [P, GT]) for i in range(2)]
        xT = [sb(f"xT{i}", [P, GT]) for i in range(2)]
        stats1 = sb("stats1", [P, NT, 6])
        after_stats = sb("after_stats", [P, 1])
        mv1 = sb("mv1", [P, NT, 2])
        var1 = sb("var1", [P, NT])
        r1 = sb("r1", [P, NT])
        power = sb("power", [P, NT])
        xn = sb("xn", [P, NT, D])
        xnT = sb("xnT", [P, GT])
        qf = sb("qf", [P, GT])
        kf = sb("kf", [P, GT])
        rest_q = sb("rest_q", [P, GT])
        rest_k = sb("rest_k", [P, GT])
        qp = sb("qp", [P, PARTS, GT], BF16)
        kp = sb("kp", [P, PARTS, GT], BF16)
        Qs = [sb(f"Qs{i}", [P, PAIRS, GT], BF16) for i in range(2)]
        Kn = sb("Kn", [ROWS, PAIRS, GT], BF16)
        Ks = [sb(f"Ks{i}", [P, PAIRS, GB, 2, S], BF16) for i in range(2)]
        neg_max = sb("neg_max", [P, NT, H])
        neg_rest = sb("neg_rest", [P, NT, H])
        neg_parts = sb("neg_parts", [P, NT, P], BF16)
        shiftT = sb("shiftT", [H * PARTS, GT], BF16)
        probs = sb("probs", [P, PAIRS, GT])
        Vs = [sb(f"Vs{i}", [P, GB, PAIRS, 32]) for i in range(2)]
        inv_den = sb("inv_den", [P, GT])
        attnT = sb("attnT", [P, GT])
        x1 = [sb(f"x1_{i}", [P, NT, DX]) for i in range(2)]
        stats2 = sb("stats2", [P, NT, 6])
        mv2 = sb("mv2", [P, NT, 2])
        var2 = sb("var2", [P, NT])
        r2 = sb("r2", [P, NT])
        top = sb("top", [P, 4, NT])
        ga = sb("ga", [P, NT, E])
        gb = sb("gb", [P, NT, E])
        first = sb("first", [P, NT, E])
        gc = sb("gc", [P, NT, E])
        logits = sb("logits", [P, G * NT * E])
        picked = sb("picked", [P, G * NT * E], BF16)
        counts = sb("counts", [P, E])
        keep = sb("keep", [P, E])
        any_keep = sb("any_keep", [P, 1])
        any_keep_i = sb("any_keep_i", [P, 1], I32)
        w1s = sb("w1s", [P, E, D])
        w2s = sb("w2s", [P, E, D])
        b1s = sb("b1s", [P, E])
        b2s = sb("b2s", [1, E, D])
        one_row = sb("one_row", [1, P])
        xe = sb("xe", [P, NT, D])
        xe_n = sb("xe_n", [P, NT, D])
        xeT = sb("xeT", [P, GT])
        hidden = [sb(f"hidden{i}", [P, GT]) for i in range(2)]
        comb = sb("comb", [P, NT, E])
        esum = sb("esum", [P, NT])

        st = [ps("st0"), ps("st1")]
        sc = [ps("sc0"), ps("sc1")]
        o_ps = ps("o_ps")
        den_ps = ps("den_ps")
        xb = [ps("xb0"), ps("xb1")]

        w_in = sem("w_in")
        c_in = sem("c_in")
        ones_in = [sem("ones_in0"), sem("ones_in1")]
        x_in = [sem("x_in0"), sem("x_in1")]
        ctx_in = [sem("ctx_in0"), sem("ctx_in1")]
        xt_in = [sem("xt_in0"), sem("xt_in1")]
        q_in = [sem("q_in0"), sem("q_in1")]
        k_in = sem("k_in")
        k_blocks = sem("k_blocks")
        shift_in = sem("shift_in")
        k_out = sem("k_out")
        q_out = sem("q_out")
        x1_free = [sem("x1_free0"), sem("x1_free1")]
        setup_dve = sem("setup_dve")
        setup_pe = sem("setup_pe")
        vs_zero = sem("vs_zero")
        ln1_chain = sem("ln1_chain")
        ln1_done = sem("ln1_done")
        power_set = sem("power_set")
        r1_done = sem("r1_done")
        xn_done = sem("xn_done")
        xnT_mm = sem("xnT_mm")
        xnT_done = sem("xnT_done")
        k_mm = sem("k_mm")
        k_copied = sem("k_copied")
        q_mm = sem("q_mm")
        q_copied = sem("q_copied")
        k_chain = sem("k_chain")
        q_chain = sem("q_chain")
        k_parts = sem("k_parts")
        q_parts = sem("q_parts")
        v_mm = sem("v_mm")
        v_done = sem("v_done")
        s_mm = sem("s_mm")
        max_done = sem("max_done")
        neg_chain = sem("neg_chain")
        neg_zero = sem("neg_zero")
        neg_done = sem("neg_done")
        shift_mm = sem("shift_mm")
        shift_copied = sem("shift_copied")
        st_mm = sem("st_mm")
        exp_done = sem("exp_done")
        half_mm = sem("half_mm")
        norm_chain = sem("norm_chain")
        norm_done = sem("norm_done")
        mix_mm = sem("mix_mm")
        x1_done = sem("x1_done")
        gate_chain = sem("gate_chain")
        gates_done = sem("gates_done")
        count_mm = sem("count_mm")
        count_chain = sem("count_chain")
        keep_known = sem("keep_known")
        ew_in = sem("ew_in")
        xe_in = sem("xe_in")
        e_chain = sem("e_chain")
        var2_done = sem("var2_done")
        r2_done = sem("r2_done")
        xe_done = sem("xe_done")
        xeT_mm = sem("xeT_mm")
        xeT_done = sem("xeT_done")
        hid_mm = sem("hid_mm")
        hid_done = sem("hid_done")
        y_mm = sem("y_mm")
        y_added = sem("y_added")
        e_exp = sem("e_exp")
        e_sub = sem("e_sub")
        e_stored = sem("e_stored")

        ident = cst[:, C_IDENT:C_IDENT + P]
        rhs_x = cst[:, C_IDENT:C_IDENT + DX]
        rhs_attn = wts[:, W_OT:W_OT + DX]
        desc = cst[:, C_DESC:C_DESC + NT * E].rearrange("p (t e) -> p t e", e=E)
        x_dram = x_nat.rearrange("(g t p) d -> g p t d", t=NT, p=P)
        out_dram = out.rearrange("(g t p) d -> g p t d", t=NT, p=P)

        def wide(col):
            return col.unsqueeze(2).to_broadcast([P, NT, E])

        q_scratch, k_scratch = ([nc.dram_tensor(f"{n}_scratch{i}", (P, PARTS, GT), BF16, kind="Internal").ap()
                                 for i in range(2)] for n in "qk")
        q_rows = [s.rearrange("(p r) c n -> r p c n", r=2 * DK) for s in q_scratch]
        k_rows = [s.rearrange("(p r) c n -> r p c n", r=2 * DK) for s in k_scratch]

        block = ctx.enter_context(nc.Block())

        def nr(i, u):
            return i * 2 + u

        @block.sync
        def _(sp):
            def load_inputs(i, u, free=True):
                g = nr(i, u)
                if free:
                    sp.wait_ge(xn_done, g - 1)
                sp.dma_start(xin[u][:], x_dram[g]).then_inc(x_in[u], 16)
                if free:
                    sp.wait_ge(v_mm, g - 1)
                sp.dma_start(ctxT[u][:], ctx_t[g]).then_inc(ctx_in[u], 16)

            def load_xt(i, u, free=True):
                g = nr(i, u)
                if free:
                    sp.wait_ge(mix_mm, 2 * (g - 1))
                sp.dma_start(xT[u][:], x_t[g]).then_inc(xt_in[u], 16)

            def spread(i, u):
                g = nr(i, u)
                sp.wait_ge(k_parts, g + 1)
                sp.dma_start(k_scratch[u], kp[:]).then_inc(k_out, 16)
                sp.wait_ge(q_parts, g + 1)
                sp.dma_start(q_scratch[u], qp[:]).then_inc(q_out, 16)
                sp.wait_ge(k_out, 16 * (g + 1))
                sp.wait_ge(k_blocks, g)
                for t, (_, part) in enumerate(PRODUCTS):
                    row = 2 * t * DK
                    sp.dma_start(Kn[row:row + 2 * DK, :, :], k_rows[u][:, :, part, :]).then_inc(k_in, 16)
                sp.wait_ge(q_out, 16 * (g + 1))
                for t, (part, _) in enumerate(PRODUCTS):
                    row = 2 * t * DK
                    sp.dma_start(Qs[u][row:row + 2 * DK, :, :], q_rows[u][:, :, part, :]).then_inc(q_in[u], 16)

            def shift_rows(i, u):
                g = nr(i, u)
                sp.wait_ge(shift_copied, g + 1)
                for p in range(PAIRS):
                    sp.dma_start(Qs[u][ROWS:ROWS + SHIFT_ROWS, p, :],
                                 shiftT[p * SHIFT_ROWS:(p + 1) * SHIFT_ROWS, :]).then_inc(shift_in, 16)

            def store(i, u):
                g = nr(i, u)
                sp.wait_ge(x1_done, 2 * (g + 1))
                sp.dma_start(out_dram[g], x1[u][:, :, 0:D]).then_inc(x1_free[u], 16)

            sp.dma_start(ctxT[0][:], ctx_t[0]).then_inc(ctx_in[0], 16)
            sp.dma_start(wts[:], weights).then_inc(w_in, 16)
            sp.dma_start(xin[0][:], x_dram[0]).then_inc(x_in[0], 16)
            sp.dma_start(cst[:], consts).then_inc(c_in, 16)
            sp.dma_start(identb[:], ident_b).then_inc(c_in, 16)
            for u in range(2):
                sp.dma_start(Ks[u][ROWS:ROWS + SHIFT_ROWS, :, :, :, :], shift_ones).then_inc(ones_in[u], 16)
            load_inputs(0, 1, free=False)
            load_xt(0, 0, free=False)
            load_xt(0, 1, free=False)
            spread(0, 0)
            shift_rows(0, 0)
            spread(0, 1)
            with sp.Fori(0, G // 2 - 1) as i:
                load_inputs(i + 1, 0)
                shift_rows(i, 1)
                store(i, 0)
                spread(i + 1, 0)
                load_inputs(i + 1, 1)
                load_xt(i + 1, 0)
                shift_rows(i + 1, 0)
                store(i, 1)
                spread(i + 1, 1)
                load_xt(i + 1, 1)
            last = G // 2 - 1
            shift_rows(last, 1)
            store(last, 0)
            store(last, 1)
            for u in range(2):
                sp.wait_ge(x1_free[u], 16 * (G // 2 + 1))
            sp.wait_ge(keep_known, 1)
            go = sp.value_load(any_keep_i[0:1, 0:1], min_val=0, max_val=1)
            with sp.If(go > 0):
                for dst, src in ((w1s[:], w1), (w2s[:], w2), (b1s[:], b1_t), (b2s[:], b2_rows)):
                    sp.dma_start(dst, src).then_inc(ew_in, 16)
                sp.dma_start(xe[:], out_dram[0]).then_inc(xe_in, 16)
                with sp.Fori(0, G - 1) as g:
                    sp.wait_ge(y_added, NT * E * (g + 1))
                    sp.dma_start(out_dram[g], xe[:]).then_inc(e_stored, 16)
                    sp.wait_ge(e_stored, 16 * (g + 1))
                    sp.dma_start(xe[:], out_dram[g + 1]).then_inc(xe_in, 16)
                sp.wait_ge(y_added, NT * E * G)
                sp.dma_start(out_dram[G - 1], xe[:]).then_inc(e_stored, 16)
                sp.wait_ge(e_stored, 16 * G)

        @block.gpsimd
        def _(pool):
            def normalise(i, u):
                g = nr(i, u)
                pool.wait_ge(ln1_done, g + 1)
                pool.wait_ge(xnT_mm, g)
                inverse_root(var1, r1, r1_done)
                pool.wait_ge(power_set, 1)
                pool.wait_ge(r1_done, g + 1)
                for t in range(NT):
                    last = pool.tensor_scalar(xn[:, t, :], xin[u][:, t, :], mv1[:, t, 0:1], r1[:, t:t + 1],
                                              ALU.subtract, ALU.mult)
                last.then_inc(xn_done, 1)

            def inverse_root(var, r, done):
                pool.tensor_tensor(r[:, :], var[:, :], power[:, :], ALU.pow).then_inc(done, 1)

            def parts(i, u, copied, full, rest, pieces, chain_sem, done):
                g = nr(i, u)
                pool.wait_ge(copied, 2 * (g + 1))
                c = Chain(pool, chain_sem, g)
                pool.tensor_tensor(rest[:, :], full[:, :], pieces[:, 0, :], ALU.subtract)
                c.link(pool.tensor_tensor(pieces[:, 1, :], full[:, :], pieces[:, 0, :], ALU.subtract))
                pool.tensor_tensor(pieces[:, 2, :], rest[:, :], pieces[:, 1, :], ALU.subtract).then_inc(done, 1)

            def parts_k(i, u):
                parts(i, u, k_copied, kf, rest_k, kp, k_chain, k_parts)

            def parts_q(i, u):
                parts(i, u, q_copied, qf, rest_q, qp, q_chain, q_parts)

            pool.memset(power[:, :], -0.5).then_inc(power_set, 1)
            pool.wait_ge(power_set, 1)
            normalise(0, 0)
            parts_k(0, 0)
            parts_q(0, 0)
            for u in range(2):
                pool.memset(Vs[u][:], 0.0).then_inc(vs_zero, 1)
            normalise(0, 1)
            parts_k(0, 1)
            parts_q(0, 1)
            with pool.Fori(0, G // 2 - 1) as i:
                for u in range(2):
                    normalise(i + 1, u)
                    parts_k(i + 1, u)
                    parts_q(i + 1, u)
            pool.wait_ge(keep_known, 1)
            go = pool.value_load(any_keep_i[0:1, 0:1], min_val=0, max_val=1)
            with pool.If(go > 0):
                with pool.Fori(0, G) as g:
                    pool.wait_ge(var2_done, g + 1)
                    inverse_root(var2, r2, r2_done)

        @block.scalar
        def _(act):
            def copy_xnT(i, u):
                act.wait_ge(xnT_mm, nr(i, u) + 1)
                act.activation(xnT[:, :], xb[1][:, :], ACT.Copy).then_inc(xnT_done, 1)

            def copy_k(i, u, free=True):
                g = nr(i, u)
                act.wait_ge(k_mm, g + 1)
                bias = wts[:, W_BIAS + 1:W_BIAS + 2]
                if free:
                    act.wait_ge(k_parts, g)
                act.activation(kf[:, :], xb[0][:, :], ACT.Identity, bias=bias).then_inc(k_copied, 1)
                if free:
                    act.wait_ge(k_out, 16 * g)
                act.activation(kp[:, 0, :], xb[0][:, :], ACT.Identity, bias=bias).then_inc(k_copied, 1)

            def copy_q(i, u, free=True):
                g = nr(i, u)
                act.wait_ge(q_mm, g + 1)
                bias = wts[:, W_BIAS:W_BIAS + 1]
                if free:
                    act.wait_ge(q_parts, g)
                act.activation(qf[:, :], xb[0][:, :], ACT.Identity, bias=bias).then_inc(q_copied, 1)
                if free:
                    act.wait_ge(q_out, 16 * g)
                act.activation(qp[:, 0, :], xb[0][:, :], ACT.Identity, bias=bias).then_inc(q_copied, 1)

            def exps(i, u, s):
                g = nr(i, u)
                act.wait_ge(st_mm, PAIRS * g + s + 1)
                act.activation(probs[:, ORDER[s], :], st[s % 2][:, :], ACT.Exp, scale=SCALE).then_inc(exp_done, 1)

            copy_k(0, 0, free=False)
            copy_xnT(0, 0)
            copy_q(0, 0, free=False)
            copy_k(0, 1)
            copy_xnT(0, 1)
            copy_q(0, 1)

            def step(i, u, ahead=True):
                for s in range(7):
                    exps(i, u, s)
                if ahead:
                    copy_xnT(i + 1, u)
                exps(i, u, 7)
                if ahead:
                    copy_k(i + 1, u)
                    copy_q(i + 1, u)

            with act.Fori(0, G // 2 - 1) as i:
                step(i, 0)
                step(i, 1)
            step(G // 2 - 1, 0, ahead=False)
            step(G // 2 - 1, 1, ahead=False)
            act.wait_ge(keep_known, 1)
            go = act.value_load(any_keep_i[0:1, 0:1], min_val=0, max_val=1)
            with act.If(go > 0):
                act.wait_ge(ew_in, 64)
                with act.Fori(0, G) as g:
                    act.wait_ge(e_sub, g + 1)
                    act.activation(comb[:], ga[:], ACT.Exp).then_inc(e_exp, 1)
                    act.wait_ge(xeT_mm, g + 1)
                    act.activation(xeT[:, :], xb[1][:, :], ACT.Copy).then_inc(xeT_done, 1)
                    for e in range(E):
                        act.wait_ge(hid_mm, E * g + e + 1)
                        act.activation(hidden[e % 2][:, :], xb[0][:, :], ACT.Relu,
                                       bias=b1s[:, e:e + 1]).then_inc(hid_done, 1)

        @block.vector
        def _(dve):
            def row_stats(chain, stats, mv, var, rows):
                for t in range(NT):
                    ins = dve.bn_stats(stats[:, t, :], rows[:, t, 0:D])
                chain.link(ins)
                dve.memset(after_stats[:, :], 0.0)
                for t in range(NT):
                    ins = dve.bn_aggr(mv[:, t, :], stats[:, t, :])
                chain.link(ins)
                return dve.tensor_scalar(var[:, :], mv[:, :, 1], EPS, None, ALU.add)

            def ln1(i, u):
                g = nr(i, u)
                dve.wait_ge(x_in[u], 16 * (i + 1))
                dve.wait_ge(xn_done, g)
                c = Chain(dve, ln1_chain, 2 * g)
                row_stats(c, stats1, mv1, var1, xin[u]).then_inc(ln1_done, 1)

            def copy_v(i, u):
                g = nr(i, u)
                dve.wait_ge(v_mm, g + 1)
                for hh in range(2):
                    rows = slice(hh * S, (hh + 1) * S)
                    src = xb[0][rows, :].rearrange("k (b j q d) -> k (b j) q d", b=GB, q=2, d=DK)
                    for q in range(2):
                        col = q * 2 * DK + hh * DK
                        dst = Vs[u][rows, :, q::2, col:col + DK]
                        last = dve.tensor_copy(dst.rearrange("k b j d -> k b j d"),
                                               src[:, :, q, :].rearrange("k (b j) d -> k b j d", b=GB))
                last.then_inc(v_done, 1)

            def block_k(i, u):
                g = nr(i, u)
                dve.wait_ge(k_in, SPREADS * (g + 1))
                for hh in range(2):
                    last = dve.tensor_scalar(Ks[u][0:ROWS, :, :, hh, :],
                                             Kn[:, :, :].rearrange("r p (b k) -> r p b k", k=S),
                                             cst[0:ROWS, C_MASK + hh:C_MASK + hh + 1], None, ALU.mult)
                last.then_inc(k_blocks, 1)

            def row_max(i, u, t):
                dve.wait_ge(s_mm, NT * nr(i, u) + t + 1)
                for n in range(2):
                    last = dve.tensor_reduce(neg_max[:, t, 8 * n:8 * n + 8],
                                             sc[n][:, :].rearrange("q (h k) -> q h k", k=S), AX.X, ALU.max,
                                             negate=True)
                last.then_inc(max_done, 1)

            def neg_part(n):
                return neg_parts[:, :, 0:H * PARTS].rearrange("q t (h r) -> q t h r", r=PARTS)[:, :, :, n]

            def shift_parts(i, u):
                g = nr(i, u)
                dve.wait_ge(max_done, NT * (g + 1))
                c = Chain(dve, neg_chain, 2 * g)
                c.link(dve.tensor_copy(neg_part(0), neg_max[:]))
                dve.tensor_tensor(neg_rest[:], neg_max[:], neg_part(0), ALU.subtract)
                c.link(dve.tensor_tensor(neg_part(1), neg_max[:], neg_part(0), ALU.subtract))
                dve.tensor_tensor(neg_part(2), neg_rest[:], neg_part(1), ALU.subtract).then_inc(neg_done, 1)

            def copy_shift(i, u):
                g = nr(i, u)
                dve.wait_ge(shift_mm, g + 1)
                dve.wait_ge(shift_in, 16 * PAIRS * g)
                dve.tensor_copy(shiftT[:, :], xb[1][0:H * PARTS, 0:GT // 2].bitcast(BF16)).then_inc(shift_copied, 1)

            def quotients(i, u):
                g = nr(i, u)
                dve.wait_ge(half_mm, 2 * (g + 1))
                c = Chain(dve, norm_chain, g)
                c.link(dve.reciprocal(inv_den[:, :], den_ps[:, :]))
                dve.tensor_tensor(attnT[:, :], o_ps[:, :], inv_den[:, :], ALU.mult).then_inc(norm_done, 1)

            def gates(i, u):
                g = nr(i, u)
                dve.wait_ge(x1_free[u], 16 * (i + 1))
                for n in range(2):
                    dve.wait_ge(mix_mm, 2 * g + n + 1)
                    dve.tensor_tensor(x1[u][:, 2 * n:2 * n + 2, :],
                                      sc[n][:, 0:2 * DX].rearrange("p (t d) -> p t d", d=DX),
                                      bias_row[:, :].unsqueeze(1).to_broadcast([P, 2, DX]),
                                      ALU.add).then_inc(x1_done, 1)
                dve.wait_ge(x1_done, 2 * (g + 1))
                c = Chain(dve, gate_chain, 12 * g)
                lo = logits[:, bass.ds(g * (NT * E), NT * E)]
                c.link(dve.tensor_copy(ga[:], x1[u][:, :, D:DX]))
                dve.tensor_copy(lo.rearrange("p (t e) -> p t e", e=E), x1[u][:, :, D:DX])
                pick(c, ga, top[:, 0, :], top[:, 1, :], first)
                c.link(dve.scalar_tensor_tensor(out=gb[:], in0=first[:], scalar=-1e30, in1=ga[:],
                                                op0=ALU.mult, op1=ALU.add))
                pick(c, gb, top[:, 2, :], top[:, 3, :], gc)
                dve.tensor_tensor(picked[:, bass.ds(g * (NT * E), NT * E)], first[:].rearrange("p t e -> p (t e)"),
                                  gc[:].rearrange("p t e -> p (t e)"), ALU.add).then_inc(gates_done, 1)
                assert c.n == 12, c.n

            def pick(c, src, best, lead, chosen):
                c.link(dve.tensor_reduce(best, src[:], AX.X, ALU.max))
                c.link(dve.tensor_tensor(chosen[:], src[:], wide(best), ALU.is_equal))
                c.link(dve.tensor_tensor(chosen[:], chosen[:], desc, ALU.mult))
                c.link(dve.tensor_reduce(lead, chosen[:], AX.X, ALU.max))
                c.link(dve.tensor_tensor(chosen[:], chosen[:], wide(lead), ALU.is_equal))

            dve.wait_ge(w_in, 16)
            ln1(0, 0)
            dve.memset(neg_parts[:], 0.0).then_inc(neg_zero, 1)
            for u in range(2):
                dve.memset(x1[u][:, 0, 0:1], 0.0).then_inc(x1_free[u], 16)
            dve.memset(onesb[:], 1.0).then_inc(setup_dve, 1)
            dve.memset(one_row[:], 1.0).then_inc(setup_dve, 1)
            dve.wait_ge(w_in, 16)
            dve.tensor_copy(bv_wide[:], wts[:, W_BIAS + 2:W_BIAS + 3].to_broadcast([P, P])).then_inc(setup_dve, 1)
            dve.tensor_copy(bo_wide[:], wts[:, W_BIAS + 3:W_BIAS + 4].to_broadcast([P, P])).then_inc(setup_dve, 1)
            ln1(0, 1)
            dve.wait_ge(setup_pe, 1)
            dve.tensor_copy(cst[:, C_IDENT + P:C_IDENT + DX], st[0][:, 0:E]).then_inc(setup_dve, 1)
            dve.wait_ge(setup_pe, 2)
            dve.tensor_copy(wts[:, W_OT + D:W_OT + DX], st[1][:, 0:E]).then_inc(setup_dve, 1)
            dve.wait_ge(setup_pe, 3)
            dve.tensor_copy(bias_row[:, :], st[0][:, 0:DX]).then_inc(setup_dve, 1)
            dve.wait_ge(vs_zero, 2)
            copy_v(0, 0)
            dve.wait_ge(c_in, 32)
            block_k(0, 0)
            for t in range(NT):
                row_max(0, 0, t)
            dve.wait_ge(neg_zero, 1)
            shift_parts(0, 0)
            copy_shift(0, 0)

            def step(i, u, last=False, ahead=True):
                nxt = (i, 1) if u == 0 else (i + 1, 0)
                if not last:
                    copy_v(*nxt)
                if ahead:
                    ln1(i + 1, u)
                if not last:
                    block_k(*nxt)
                    for t in range(NT):
                        row_max(*nxt, t)
                    shift_parts(*nxt)
                    copy_shift(*nxt)
                quotients(i, u)
                gates(i, u)

            with dve.Fori(0, G // 2 - 1) as i:
                step(i, 0)
                step(i, 1)
            step(G // 2 - 1, 0, ahead=False)
            step(G // 2 - 1, 1, last=True, ahead=False)

            dve.wait_ge(count_mm, 1)
            c = Chain(dve, count_chain, 0)
            c.link(dve.tensor_reduce(counts[:, :], st[0][:, 0:G * NT * E].rearrange("p (t e) -> p e t", e=E),
                                     AX.X, ALU.add))
            c.link(dve.tensor_scalar(keep[:, :], counts[:, :], float(CAP), None, ALU.is_le))
            c.link(dve.tensor_reduce(any_keep[:, :], keep[:, :], AX.X, ALU.max))
            dve.tensor_copy(any_keep_i[:, :], any_keep[:, :]).then_inc(keep_known, 1)
            dve.wait_ge(keep_known, 1)
            go = dve.value_load(any_keep_i[0:1, 0:1], min_val=0, max_val=1)
            with dve.If(go > 0):
                with dve.Fori(0, G) as g:
                    mine = bass.ds(g * (NT * E), NT * E)
                    c = Chain(dve, e_chain, 9 * g)
                    dve.wait_ge(xe_in, 16 * (g + 1))
                    row_stats(c, stats2, mv2, var2, xe).then_inc(var2_done, 1)
                    dve.wait_ge(r2_done, g + 1)
                    c.link(dve.tensor_tensor(gb[:], logits[:, mine].rearrange("p (t e) -> p t e", e=E),
                                             wide(r2[:, :]), ALU.mult))
                    c.link(dve.tensor_reduce(top[:, 0, :], gb[:], AX.X, ALU.max))
                    dve.tensor_tensor(ga[:], gb[:], wide(top[:, 0, :]), ALU.subtract).then_inc(e_sub, 1)
                    dve.wait_ge(e_exp, g + 1)
                    c.link(dve.tensor_reduce(esum[:, :], comb[:], AX.X, ALU.add))
                    c.link(dve.reciprocal(esum[:, :], esum[:, :]))
                    c.link(dve.tensor_tensor(comb[:], comb[:], wide(esum[:, :]), ALU.mult))
                    c.link(dve.tensor_tensor(comb[:], comb[:],
                                             picked[:, mine].rearrange("p (t e) -> p t e", e=E), ALU.mult))
                    c.link(dve.tensor_tensor(comb[:], comb[:],
                                             keep[:, :].unsqueeze(1).to_broadcast([P, NT, E]), ALU.mult))
                    assert c.n == 9
                    for t in range(NT):
                        ins = dve.tensor_scalar(xe_n[:, t, :], xe[:, t, :], mv2[:, t, 0:1], r2[:, t:t + 1],
                                                ALU.subtract, ALU.mult)
                    ins.then_inc(xe_done, 1)
                    dve.wait_ge(xe_done, g + 1)
                    for e in range(E):
                        dve.wait_ge(y_mm, E * g + e + 1)
                        if e:
                            dve.wait_ge(y_added, NT * E * g + NT * e)
                        for t in range(NT):
                            dve.scalar_tensor_tensor(out=xe[:, t, :], in0=st[e % 2][:, t * D:(t + 1) * D],
                                                     scalar=comb[:, t, e:e + 1], in1=xe[:, t, :],
                                                     op0=ALU.mult, op1=ALU.add).then_inc(y_added, 1)

        @block.tensor
        def _(pe):
            def k_proj(i, u):
                g = nr(i, u)
                pe.wait_ge(ctx_in[u], 16 * (i + 1))
                pe.matmul(xb[0][:, :], wts[:, W_K:W_K + D], ctxT[u][:, :], start=True, stop=True).then_inc(k_mm, 1)

            def transpose_xn(i, u):
                pe.wait_ge(xn_done, nr(i, u) + 1)
                for t in range(NT):
                    last = pe.transpose(xb[1][:, t * P:(t + 1) * P], xn[:, t, :], ident)
                last.then_inc(xnT_mm, 1)

            def q_proj(i, u):
                g = nr(i, u)
                pe.wait_ge(xnT_done, g + 1)
                pe.wait_ge(k_copied, 2 * (g + 1))
                pe.matmul(xb[0][:, :], wts[:, W_Q:W_Q + D], xnT[:, :], start=True, stop=True).then_inc(q_mm, 1)

            def v_proj(i, u):
                for b in range(GB):
                    for hh in range(2):
                        last = pe.matmul(xb[0][hh * S:(hh + 1) * S, b * 64:(b + 1) * 64],
                                         ctxT[u][:, b * S:(b + 1) * S], wts[:, W_V + hh * 64:W_V + (hh + 1) * 64],
                                         start=True, stop=True)
                last.then_inc(v_mm, 1)

            def scores(i, u, t):
                for b in range(2):
                    for p in range(PAIRS):
                        cols = slice((2 * t + b) * S, (2 * t + b + 1) * S)
                        last = pe.matmul(sc[p // 4][b * S:(b + 1) * S, (p % 4) * P:(p % 4 + 1) * P],
                                         Qs[u][0:ROWS, p, cols], Ks[u][0:ROWS, p, 2 * t + b, :, :], start=True, stop=True)
                last.then_inc(s_mm, 1)

            def transpose_shift(i, u):
                pe.wait_ge(c_in, 32)
                pe.wait_ge(neg_done, nr(i, u) + 1)
                dst = xb[1][:, 0:GT // 2].bitcast(BF16)
                for t in range(NT):
                    last = pe.transpose(dst[:, t * P:(t + 1) * P],
                                        neg_parts[:, t, :], identb[:, :])
                last.then_inc(shift_mm, 1)

            def scores_t(i, u, s):
                g = nr(i, u)
                if s == 0:
                    pe.wait_ge(shift_in, 16 * PAIRS * (g + 1))
                if s >= 2:
                    pe.wait_ge(exp_done, PAIRS * g + s - 1)
                p = ORDER[s]
                for b in range(GB):
                    cols = slice(b * S, (b + 1) * S)
                    last = pe.matmul(st[s % 2][:, cols], Ks[u][0:ROWS + SHIFT_ROWS, p, b, :, :],
                                     Qs[u][0:ROWS + SHIFT_ROWS, p, cols], start=True, stop=True)
                last.then_inc(st_mm, 1)

            def weigh(i, u, half, batches):
                g = nr(i, u)
                if batches[0] == 0:
                    pe.wait_ge(exp_done, PAIRS * g + HALF * (half + 1))
                    if half == 0:
                        pe.wait_ge(v_done, g + 1)
                for b in batches:
                    for s in range(half * HALF, (half + 1) * HALF):
                        p = ORDER[s]
                        j = p // 2
                        pe.matmul(o_ps[32 * j:32 * j + 32, b * S:(b + 1) * S], Vs[u][:, b, p, :],
                                  probs[:, p, b * S:(b + 1) * S], start=(half == 0 and b == 0),
                                  stop=(half == 1 and b == GB - 1), skip_group_check=True)

            def denominators(i, u, half):
                for s in range(half * HALF, (half + 1) * HALF):
                    p = ORDER[s]
                    j, q = p // 2, p % 2
                    last = pe.matmul(den_ps[32 * j:32 * j + 32, :], cst[:, C_ONES + 32 * q:C_ONES + 32 * q + 32],
                                     probs[:, p, :], start=(half == 0), stop=(half == 1), skip_group_check=True)
                last.then_inc(half_mm, 1)

            def mix(i, u):
                g = nr(i, u)
                pe.wait_ge(norm_done, g + 1)
                pe.wait_ge(xt_in[u], 16 * (i + 1))
                for t in range(NT):
                    dst = sc[t // 2][:, (t % 2) * DX:(t % 2 + 1) * DX]
                    pe.matmul(dst, attnT[:, t * P:(t + 1) * P], rhs_attn, start=True, stop=False)
                    last = pe.matmul(dst, xT[u][:, t * P:(t + 1) * P], rhs_x, start=False, stop=True)
                    if t % 2:
                        last.then_inc(mix_mm, 1)

            pe.wait_ge(w_in, 16)
            k_proj(0, 0)
            pe.wait_ge(c_in, 32)
            pe.matmul(st[0][:, 0:E], cst[:, C_CENTRE:C_CENTRE + P], wts[:, W_G:W_G + E],
                      start=True, stop=True).then_inc(setup_pe, 1)
            transpose_xn(0, 0)
            pe.wait_ge(setup_dve, 5)
            pe.matmul(st[1][:, 0:E], wts[:, W_ON:W_ON + D], cst[:, C_IDENT + P:C_IDENT + DX],
                      start=True, stop=True).then_inc(setup_pe, 1)
            q_proj(0, 0)
            pe.wait_ge(setup_dve, 6)
            pe.matmul(st[0][:, 0:DX], bv_wide[:, :], rhs_attn, start=True, stop=False)
            pe.matmul(st[0][:, 0:DX], bo_wide[:, :], rhs_x, start=False, stop=True).then_inc(setup_pe, 1)
            pe.wait_ge(q_copied, 2)
            v_proj(0, 0)
            pe.wait_ge(v_done, 1)
            k_proj(0, 1)
            transpose_xn(0, 1)
            q_proj(0, 1)
            pe.wait_ge(ones_in[0], 16)
            pe.wait_ge(ones_in[1], 16)
            pe.wait_ge(q_in[0], SPREADS)
            pe.wait_ge(k_blocks, 1)
            for t in range(NT):
                if t:
                    pe.wait_ge(max_done, t)
                scores(0, 0, t)
            transpose_shift(0, 0)
            pe.wait_ge(setup_dve, 7)

            def step(i, u, last=False, ahead=True):
                g = nr(i, u)
                nxt = (i, 1) if u == 0 else (i + 1, 0)
                near, far = range(GB // 2), range(GB // 2, GB)
                scores_t(i, u, 0)
                scores_t(i, u, 1)
                if not last:
                    pe.wait_ge(q_copied, 2 * (g + 2))
                    v_proj(*nxt)
                scores_t(i, u, 2)
                scores_t(i, u, 3)
                weigh(i, u, 0, near)
                scores_t(i, u, 4)
                weigh(i, u, 0, far)
                scores_t(i, u, 5)
                denominators(i, u, 0)

                def next_scores(t):
                    if last:
                        return
                    if t == 0:
                        pe.wait_ge(q_in[nxt[1]], SPREADS * (nxt[0] + 1))
                        pe.wait_ge(k_blocks, g + 2)
                    else:
                        pe.wait_ge(max_done, NT * (g + 1) + t)
                    scores(*nxt, t)

                next_scores(0)
                scores_t(i, u, 6)
                next_scores(1)
                if ahead:
                    pe.wait_ge(shift_copied, g + 1)
                    transpose_xn(i + 1, u)
                scores_t(i, u, 7)
                next_scores(2)
                next_scores(3)
                weigh(i, u, 1, near)
                if ahead:
                    pe.wait_ge(v_done, g + 2)
                    k_proj(i + 1, u)
                    pe.wait_ge(xnT_done, g + 3)
                if not last:
                    transpose_shift(*nxt)
                weigh(i, u, 1, far)
                denominators(i, u, 1)
                if ahead:
                    q_proj(i + 1, u)
                if not last:
                    pe.wait_ge(max_done, NT * (g + 2))
                mix(i, u)

            with pe.Fori(0, G // 2 - 1) as i:
                step(i, 0)
                step(i, 1)
            step(G // 2 - 1, 0, ahead=False)
            step(G // 2 - 1, 1, last=True, ahead=False)
            pe.wait_ge(gates_done, G)
            pe.matmul(st[0][:, 0:G * NT * E], onesb[:, :], picked[:, :], start=True, stop=True).then_inc(count_mm, 1)
            pe.wait_ge(keep_known, 1)
            go = pe.value_load(any_keep_i[0:1, 0:1], min_val=0, max_val=1)
            with pe.If(go > 0):
                pe.wait_ge(ew_in, 64)
                with pe.Fori(0, G) as g:
                    pe.wait_ge(xe_done, g + 1)
                    for t in range(NT):
                        ins = pe.transpose(xb[1][:, t * P:(t + 1) * P], xe_n[:, t, :], ident)
                    ins.then_inc(xeT_mm, 1)
                    pe.wait_ge(xeT_done, g + 1)

                    def hid(e):
                        if e:
                            pe.wait_ge(hid_done, E * g + e)
                        pe.matmul(xb[0][:, :], w1s[:, e, :], xeT[:, :], start=True, stop=True).then_inc(hid_mm, 1)

                    hid(0)
                    for e in range(E):
                        pe.wait_ge(hid_done, E * g + e + 1)
                        if e + 1 < E:
                            hid(e + 1)
                        if e >= 2:
                            pe.wait_ge(y_added, NT * E * g + NT * (e - 1))
                        for t in range(NT):
                            dst = st[e % 2][:, t * D:(t + 1) * D]
                            pe.matmul(dst, hidden[e % 2][:, t * P:(t + 1) * P], w2s[:, e, :], start=True, stop=False)
                            ins = pe.matmul(dst, one_row[:, :], b2s[:, e, :], start=False, stop=True)
                        ins.then_inc(y_mm, 1)


def kernel(**inputs):
    import ml_dtypes
    import numpy as np
    import concourse.bacc as bacc
    from concourse.bass_utils import run_bass_kernel_spmd

    a = {k: np.asarray(v) for k, v in inputs.items()}
    x = np.ascontiguousarray(a["x"].reshape(TOK, D))
    ctx = a["ctx_1024"].reshape(TOK, D)

    def by_group(m):
        return np.ascontiguousarray(m.reshape(G, GT, D).transpose(0, 2, 1))

    w = np.zeros((D, W_COLS), np.float32)
    w[:, W_Q:W_Q + D] = a["L0_xattn_Wq"].T
    w[:, W_K:W_K + D] = a["L0_xattn_Wk"].T
    w[:, W_V:W_V + D] = a["L0_xattn_Wv"].reshape(PAIRS, 2, DK, D).transpose(3, 1, 0, 2).reshape(D, D)
    w[:, W_OT:W_OT + D] = a["L0_xattn_Wo"].T
    w[:, W_ON:W_ON + D] = a["L0_xattn_Wo"]
    w[:, W_G:W_G + E] = a["L0_ffn_gate_w"].T
    for n, name in enumerate(("bq", "bk", "bv", "bo")):
        w[:, W_BIAS + n] = a["L0_xattn_" + name]
    c = np.zeros((P, C_COLS), np.float32)
    c[:, C_IDENT:C_IDENT + P] = np.eye(P)
    c[:, C_CENTRE:C_CENTRE + P] = np.eye(P) - 1.0 / D
    for q in range(2):
        for hh in range(2):
            first = C_ONES + 32 * q + 16 * q + 8 * hh
            c[hh * S:(hh + 1) * S, first:first + DK] = 1.0
    c[:, C_DESC:C_DESC + NT * E] = np.tile(np.arange(E, 0, -1), NT)
    for hh in range(2):
        c[:ROWS, C_MASK + hh] = np.arange(ROWS) // DK % 2 == hh
    ones = np.zeros((SHIFT_ROWS, PAIRS, GB, 2, S), ml_dtypes.bfloat16)
    for hh in range(2):
        ones[hh * PARTS:(hh + 1) * PARTS, :, :, hh] = 1.0
    arrays = {
        "x_nat": x, "x_t": by_group(x), "ctx_t": by_group(ctx), "weights": w, "consts": c, "shift_ones": ones,
        "ident_b": np.eye(P).astype(ml_dtypes.bfloat16),
        "w1": np.ascontiguousarray(a["L0_ffn_W1"].transpose(1, 0, 2)),
        "w2": np.ascontiguousarray(a["L0_ffn_W2"].transpose(1, 0, 2)),
        "b1_t": np.ascontiguousarray(a["L0_ffn_b1"].T),
        "b2_rows": np.ascontiguousarray(a["L0_ffn_b2"].reshape(1, E, D)),
    }
    nc = bacc.Bacc("TRN2", target_bir_lowering=False, num_devices=1)
    aps = [nc.dram_tensor(n, v.shape, mybir.dt.from_np(v.dtype), kind="ExternalInput").ap()
           for n, v in arrays.items()]
    out = nc.dram_tensor("out", (TOK, D), F32, kind="ExternalOutput").ap()
    build(nc, *aps, out)
    r = run_bass_kernel_spmd(nc, [arrays], core_ids=[0])
    return r.results[0]["out"].reshape(B, S, D)
```

```python
from contextlib import ExitStack

import concourse.bass as bass
from concourse import mybir

F32 = mybir.dt.float32
BF16 = mybir.dt.bfloat16
I32 = mybir.dt.int32
ALU = mybir.AluOpType
ACT = mybir.ActivationFunctionType
AX = mybir.AxisListType

B, S, D = 64, 64, 128
H, DK = 16, 8
E = 8
TOK = B * S
P = 128
GT = 512
GB = GT // S
G = TOK // GT
NT = GT // P
PAIRS = H // 2
CAP = int(1.25 * TOK / E)
EPS = 1e-5
SCALE = DK ** -0.5
PARTS = 3
PRODUCTS = [(0, 0), (0, 1), (1, 0), (0, 2), (1, 1), (2, 0)]
Q_SLOT, K_SLOT = [0, 1, 2], [1, 0, 2]


def runs(slots):
    out = []
    for t, slot in enumerate(slots):
        if out and slot == out[-1][1] + out[-1][2]:
            out[-1] = (*out[-1][:2], out[-1][2] + 1)
        else:
            out.append((t, slot, 1))
    return out


Q_RUNS = runs([Q_SLOT[a] for a, _ in PRODUCTS])
K_RUNS = runs([K_SLOT[b] for _, b in PRODUCTS])
ROWS = len(PRODUCTS) * 2 * DK
SHIFT_ROWS = 2 * PARTS
DX = D + E
ORDER = [0, 2, 4, 6, 1, 3, 5, 7]
HALF = PAIRS // 2
GATE_TILES = (G - 1) * NT
Q_SPREAD, K_SPREAD = 16 * len(Q_RUNS), 16 * len(K_RUNS)
SHIFT_COLS = 32
W_Q, W_K, W_V, W_OT, W_ON = 0, D, 2 * D, 3 * D, 3 * D + DX
W_G = W_ON + D
W_BIAS = W_G + E
W_COLS = W_BIAS + 4
C_IDENT, C_CENTRE, C_ONES = 0, DX, DX + D
C_DESC = C_ONES + 64
C_MASK = C_DESC + E
C_COLS = C_MASK + 2


LOOPS = (G - 4) // 2


class Chain:

    def __init__(self, eng, sem, base):
        self.eng, self.sem, self.base, self.n = eng, sem, base, 0

    def link(self, ins):
        ins.then_inc(self.sem, 1)
        self.n += 1
        self.eng.wait_ge(self.sem, self.base + self.n)


def build(nc, x_nat, x_t, ctx_t, weights, consts, shift_ones, ident_b, w1, w2, b1_t, b2_rows, out):
    ctx = ExitStack()
    with ctx:
        def sb(name, shape, dt=F32):
            return ctx.enter_context(nc.sbuf_tensor(name, shape, dt))

        def ps(name):
            return ctx.enter_context(nc.psum_tensor(name, [P, 512], F32))

        def sem(name):
            return ctx.enter_context(nc.semaphore(name))

        wts = sb("wts", [P, W_COLS])
        cst = sb("cst", [P, C_COLS])
        identb = sb("identb", [P, P], BF16)
        onesb = sb("onesb", [P, P], BF16)
        bv_wide = sb("bv_wide", [P, P])
        bo_wide = sb("bo_wide", [P, P])
        bias_row = sb("bias_row", [P, DX])
        xin = [sb(f"xin{i}", [P, NT, D]) for i in range(2)]
        ctxT = [sb(f"ctxT{i}", [P, GT]) for i in range(2)]
        xT = [sb(f"xT{i}", [P, GT]) for i in range(2)]
        stats1 = sb("stats1", [P, NT, 6])
        after_stats = sb("after_stats", [P, 1])
        mv1 = sb("mv1", [P, NT, 2])
        var1 = sb("var1", [P, NT])
        r1 = sb("r1", [P, NT])
        power = sb("power", [P, NT])
        xn = sb("xn", [P, NT, D])
        xnT = sb("xnT", [P, GT])
        qf = sb("qf", [P, GT])
        kf = sb("kf", [P, GT])
        rest_q = sb("rest_q", [P, GT])
        rest_k = sb("rest_k", [P, GT])
        qp = sb("qp", [P, PARTS, GT], BF16)
        kp = sb("kp", [P, PARTS, GT], BF16)
        Qs = [sb(f"Qs{i}", [P, PAIRS, GT], BF16) for i in range(2)]
        Qb = sb("Qb", [ROWS, PAIRS, GB, 2, S], BF16)
        Kn = [sb(f"Kn{i}", [ROWS, PAIRS, GT], BF16) for i in range(2)]
        Ks = [sb(f"Ks{i}", [P, PAIRS, GB, 2, S], BF16) for i in range(2)]
        neg_max = sb("neg_max", [P, GB, PAIRS])
        neg_rest = sb("neg_rest", [P, GB, PAIRS])
        neg_parts = sb("neg_parts", [P, GB, SHIFT_COLS], BF16)
        shiftT = sb("shiftT", [PARTS * PAIRS, 2, GT], BF16)
        probs = sb("probs", [P, PAIRS, GT])
        Vs = [sb(f"Vs{i}", [P, GB, PAIRS, 32]) for i in range(2)]
        inv_den = sb("inv_den", [P, GT])
        attnT = sb("attnT", [P, GT])
        x1 = [sb(f"x1_{i}", [P, NT, D]) for i in range(2)]
        stats2 = sb("stats2", [P, NT, 6])
        mv2 = sb("mv2", [P, NT, 2])
        var2 = sb("var2", [P, NT])
        r2 = sb("r2", [P, NT])
        top = sb("top", [P, 4, GATE_TILES])
        ga = sb("ga", [P, GATE_TILES, E])
        gb = sb("gb", [P, GATE_TILES, E])
        first = sb("first", [P, GATE_TILES, E])
        gc = sb("gc", [P, GATE_TILES, E])
        logits = sb("logits", [P, G * NT * E])
        picked = sb("picked", [P, G * NT * E], BF16)
        counts = sb("counts", [P, E])
        keep = sb("keep", [P, E])
        any_keep = sb("any_keep", [P, 1])
        any_keep_i = sb("any_keep_i", [P, 1], I32)
        w1s = sb("w1s", [P, E, D])
        w2s = sb("w2s", [P, E, D])
        b1s = sb("b1s", [P, E])
        b2s = sb("b2s", [1, E, D])
        one_row = sb("one_row", [1, P])
        xe = sb("xe", [P, NT, D])
        xe_n = sb("xe_n", [P, NT, D])
        xeT = sb("xeT", [P, GT])
        hidden = [sb(f"hidden{i}", [P, GT]) for i in range(2)]
        comb = sb("comb", [P, NT, E])
        esum = sb("esum", [P, NT])

        st = [ps("st0"), ps("st1")]
        sc = [ps("sc0"), ps("sc1")]
        o_ps = ps("o_ps")
        den_ps = ps("den_ps")
        xb = [ps("xb0"), ps("xb1")]

        w_in = sem("w_in")
        c_in = sem("c_in")
        ones_in = [sem("ones_in0"), sem("ones_in1")]
        x_in = [sem("x_in0"), sem("x_in1")]
        ctx_in = [sem("ctx_in0"), sem("ctx_in1")]
        xt_in = [sem("xt_in0"), sem("xt_in1")]
        q_in = [sem("q_in0"), sem("q_in1")]
        k_in = [sem("k_in0"), sem("k_in1")]
        q_blocks = sem("q_blocks")
        k_blocks = sem("k_blocks")
        shift_in = sem("shift_in")
        shift_out = sem("shift_out")
        k_out = sem("k_out")
        q_out = sem("q_out")
        x1_free = [sem("x1_free0"), sem("x1_free1")]
        setup_dve = sem("setup_dve")
        setup_pe = sem("setup_pe")
        vs_zero = sem("vs_zero")
        ln1_chain = sem("ln1_chain")
        ln1_done = sem("ln1_done")
        power_set = sem("power_set")
        r1_done = sem("r1_done")
        xn_done = sem("xn_done")
        xnT_mm = sem("xnT_mm")
        xnT_done = sem("xnT_done")
        k_mm = sem("k_mm")
        k_copied = sem("k_copied")
        q_mm = sem("q_mm")
        q_copied = sem("q_copied")
        k_chain = sem("k_chain")
        q_chain = sem("q_chain")
        k_parts = sem("k_parts")
        q_parts = sem("q_parts")
        v_mm = sem("v_mm")
        v_done = sem("v_done")
        s_mm = sem("s_mm")
        max_done = sem("max_done")
        neg_chain = sem("neg_chain")
        neg_zero = sem("neg_zero")
        neg_done = sem("neg_done")
        shift_mm = sem("shift_mm")
        shift_copied = sem("shift_copied")
        st_mm = sem("st_mm")
        qs_used = sem("qs_used")
        exp_done = sem("exp_done")
        den_mm = sem("den_mm")
        o_mm = sem("o_mm")
        norm_chain = sem("norm_chain")
        norm_done = sem("norm_done")
        mix_mm = sem("mix_mm")
        x1_done = sem("x1_done")
        gate_chain = sem("gate_chain")
        gates_done = sem("gates_done")
        count_mm = sem("count_mm")
        count_chain = sem("count_chain")
        keep_known = sem("keep_known")
        ew_in = sem("ew_in")
        xe_in = sem("xe_in")
        e_chain = sem("e_chain")
        var2_done = sem("var2_done")
        r2_done = sem("r2_done")
        xe_done = sem("xe_done")
        xeT_mm = sem("xeT_mm")
        xeT_done = sem("xeT_done")
        hid_mm = sem("hid_mm")
        hid_done = sem("hid_done")
        y_mm = sem("y_mm")
        y_added = sem("y_added")
        e_exp = sem("e_exp")
        e_sub = sem("e_sub")
        e_stored = sem("e_stored")

        ident = cst[:, C_IDENT:C_IDENT + P]
        rhs_x = cst[:, C_IDENT:C_IDENT + DX]
        rhs_attn = wts[:, W_OT:W_OT + DX]
        desc = cst[:, C_DESC:C_DESC + E]
        x_dram = x_nat.rearrange("(g t p) d -> g p t d", t=NT, p=P)
        out_dram = out.rearrange("(g t p) d -> g p t d", t=NT, p=P)

        def wide(col, tiles=NT):
            return col.unsqueeze(2).to_broadcast([P, tiles, E])

        q_scratch, k_scratch = ([nc.dram_tensor(f"{n}_scratch{i}", (PARTS, P, GT), BF16, kind="Internal").ap()
                                 for i in range(2)] for n in "qk")
        q_rows = [s.rearrange("c (r p) n -> (c r) p n", p=PAIRS) for s in q_scratch]
        k_rows = [s.rearrange("c (r p) n -> (c r) p n", p=PAIRS) for s in k_scratch]
        shift_scratch = nc.dram_tensor("shift_scratch", (2, PARTS * PAIRS, GT), BF16, kind="Internal").ap()

        block = ctx.enter_context(nc.Block())

        def nr(i, u):
            return i * 2 + u

        def after(i, u, n):
            i, u = i + (u + n) // 2, (u + n) % 2
            return (i, u) if not isinstance(i, int) or nr(i, u) < G else None

        @block.sync
        def _(sp):
            def load_x(i, u, free=True):
                g = nr(i, u)
                if free:
                    sp.wait_ge(xn_done, g - 1)
                sp.dma_start(xin[u][:], x_dram[g]).then_inc(x_in[u], 16)

            def load_ctx(i, u, free=True):
                g = nr(i, u)
                if free:
                    sp.wait_ge(v_mm, g - 1)
                sp.dma_start(ctxT[u][:], ctx_t[g]).then_inc(ctx_in[u], 16)

            def load_xt(i, u, free=True):
                g = nr(i, u)
                if free:
                    sp.wait_ge(mix_mm, 2 * (g - 1))
                sp.dma_start(xT[u][:], x_t[g]).then_inc(xt_in[u], 16)

            def write_q(i, u):
                sp.wait_ge(q_parts, nr(i, u) + 1)
                sp.dma_start(q_scratch[u].rearrange("c f n -> f c n"), qp[:]).then_inc(q_out, 16)

            def write_k(i, u):
                sp.wait_ge(k_parts, nr(i, u) + 1)
                sp.dma_start(k_scratch[u].rearrange("c f n -> f c n"), kp[:]).then_inc(k_out, 16)

            def read_q(i, u, free=True):
                g = nr(i, u)
                sp.wait_ge(q_out, 16 * (g + 1))
                if free:
                    sp.wait_ge(qs_used, g)
                spread(Qs[u], q_rows[u], Q_RUNS, q_in[u])

            def spread(dst, rows, runs_of, done):
                for t, slot, n in runs_of:
                    sp.dma_start(dst[2 * t * DK:2 * (t + n) * DK, :, :],
                                 rows[2 * slot * DK:2 * (slot + n) * DK]).then_inc(done, 16)

            def read_k(i, u):
                sp.wait_ge(k_out, 16 * (nr(i, u) + 1))
                spread(Kn[u], k_rows[u], K_RUNS, k_in[u])

            def read_shift(i, u):
                sp.wait_ge(shift_out, 16 * (nr(i, u) + 1))
                sp.dma_start(Qs[u][ROWS:ROWS + SHIFT_ROWS, :, :],
                             shift_scratch.rearrange("h (c p) n -> (h c) p n", p=PAIRS)).then_inc(shift_in, 16)

            def store(i, u):
                g = nr(i, u)
                sp.wait_ge(x1_done, 2 * (g + 2))
                sp.dma_start(out_dram[g], x1[u][:]).then_inc(x1_free[u], 16)

            sp.dma_start(ctxT[0][:], ctx_t[0]).then_inc(ctx_in[0], 16)
            sp.dma_start(wts[:], weights).then_inc(w_in, 16)
            sp.dma_start(xin[0][:], x_dram[0]).then_inc(x_in[0], 16)
            sp.dma_start(cst[:], consts).then_inc(c_in, 16)
            load_x(0, 1, free=False)
            load_ctx(0, 1, free=False)
            sp.dma_start(identb[:], ident_b).then_inc(c_in, 16)
            for u in range(2):
                sp.dma_start(Ks[u][ROWS:ROWS + SHIFT_ROWS, :, :, :, :], shift_ones).then_inc(ones_in[u], 16)
                load_xt(0, u, free=False)
            write_k(0, 0)
            read_k(0, 0)
            write_q(0, 0)
            read_q(0, 0, free=False)
            load_x(1, 0)
            load_x(1, 1)
            write_k(0, 1)
            read_k(0, 1)
            write_q(0, 1)
            read_q(0, 1, free=False)
            load_ctx(1, 0)
            read_shift(0, 0)

            def step(i, u):
                g = nr(i, u)
                one, two, three, four = (after(i, u, n) for n in range(1, 5))
                if two:
                    write_k(*two)
                    read_k(*two)
                    write_q(*two)
                if one:
                    read_shift(*one)
                if two:
                    read_q(*two)
                if three:
                    load_ctx(*three)
                if four:
                    load_x(*four)
                store(i, u)
                if two:
                    load_xt(*two)

            with sp.Fori(0, LOOPS) as i:
                step(i, 0)
                step(i, 1)
            for g in range(2 * LOOPS, G):
                step(g // 2, g % 2)
            for u in range(2):
                sp.wait_ge(x1_free[u], 16 * (G // 2 + 1))
            sp.wait_ge(keep_known, 1)
            go = sp.value_load(any_keep_i[0:1, 0:1], min_val=0, max_val=1)
            with sp.If(go > 0):
                for dst, src in ((w1s[:], w1), (w2s[:], w2), (b1s[:], b1_t), (b2s[:], b2_rows)):
                    sp.dma_start(dst, src).then_inc(ew_in, 16)
                sp.dma_start(xe[:], out_dram[0]).then_inc(xe_in, 16)
                with sp.Fori(0, G - 1) as g:
                    sp.wait_ge(y_added, NT * E * (g + 1))
                    sp.dma_start(out_dram[g], xe[:]).then_inc(e_stored, 16)
                    sp.wait_ge(e_stored, 16 * (g + 1))
                    sp.dma_start(xe[:], out_dram[g + 1]).then_inc(xe_in, 16)
                sp.wait_ge(y_added, NT * E * G)
                sp.dma_start(out_dram[G - 1], xe[:]).then_inc(e_stored, 16)
                sp.wait_ge(e_stored, 16 * G)

        @block.gpsimd
        def _(pool):
            def inverse_root1(i, u, free=True):
                g = nr(i, u)
                pool.wait_ge(ln1_done, g + 1)
                if free:
                    pool.wait_ge(xnT_mm, g)
                inverse_root(var1, r1, r1_done)

            def normalise(i, u):
                g = nr(i, u)
                pool.wait_ge(power_set, 1)
                pool.wait_ge(r1_done, g + 1)
                for t in range(NT):
                    last = pool.tensor_scalar(xn[:, t, :], xin[u][:, t, :], mv1[:, t, 0:1], r1[:, t:t + 1],
                                              ALU.subtract, ALU.mult)
                last.then_inc(xn_done, 1)

            def inverse_root(var, r, done):
                pool.tensor_tensor(r[:, :], var[:, :], power[:, :], ALU.pow).then_inc(done, 1)

            def parts(i, u, copied, full, rest, pieces, slot, chain_sem, done):
                g = nr(i, u)
                pool.wait_ge(copied, 2 * (g + 1))
                c = Chain(pool, chain_sem, g)
                part = [pieces[:, slot[n], :] for n in range(PARTS)]
                pool.tensor_tensor(rest[:, :], full[:, :], part[0], ALU.subtract)
                c.link(pool.tensor_tensor(part[1], full[:, :], part[0], ALU.subtract))
                pool.tensor_tensor(part[2], rest[:, :], part[1], ALU.subtract).then_inc(done, 1)

            def parts_k(i, u):
                parts(i, u, k_copied, kf, rest_k, kp, K_SLOT, k_chain, k_parts)

            def parts_q(i, u):
                parts(i, u, q_copied, qf, rest_q, qp, Q_SLOT, q_chain, q_parts)

            pool.memset(power[:, :], -0.5).then_inc(power_set, 1)
            pool.wait_ge(power_set, 1)
            inverse_root1(0, 0, free=False)
            parts_k(0, 0)
            inverse_root1(0, 1)
            parts_q(0, 0)
            parts_k(0, 1)
            parts_q(0, 1)
            inverse_root1(1, 0)
            for u in range(2):
                pool.memset(Vs[u][:], 0.0).then_inc(vs_zero, 1)
            normalise(1, 0)

            def step(i, u):
                two, three = after(i, u, 2), after(i, u, 3)
                if two:
                    parts_k(*two)
                    parts_q(*two)
                if three:
                    inverse_root1(*three)
                    normalise(*three)

            with pool.Fori(0, LOOPS) as i:
                step(i, 0)
                step(i, 1)
            for g in range(2 * LOOPS, G):
                step(g // 2, g % 2)
            pool.wait_ge(keep_known, 1)
            go = pool.value_load(any_keep_i[0:1, 0:1], min_val=0, max_val=1)
            with pool.If(go > 0):
                with pool.Fori(0, G) as g:
                    pool.wait_ge(var2_done, g + 1)
                    inverse_root(var2, r2, r2_done)

        @block.scalar
        def _(act):
            def copy_xnT(i, u):
                act.wait_ge(xnT_mm, nr(i, u) + 1)
                act.activation(xnT[:, :], xb[1][:, :], ACT.Copy).then_inc(xnT_done, 1)

            def copy_k(i, u, free=True):
                g = nr(i, u)
                act.wait_ge(k_mm, g + 1)
                bias = wts[:, W_BIAS + 1:W_BIAS + 2]
                if free:
                    act.wait_ge(k_parts, g)
                act.activation(kf[:, :], xb[0][:, :], ACT.Identity, bias=bias).then_inc(k_copied, 1)
                if free:
                    act.wait_ge(k_out, 16 * g)
                act.activation(kp[:, K_SLOT[0], :], xb[0][:, :], ACT.Identity, bias=bias).then_inc(k_copied, 1)

            def copy_q(i, u, free=True):
                g = nr(i, u)
                act.wait_ge(q_mm, g + 1)
                bias = wts[:, W_BIAS:W_BIAS + 1]
                if free:
                    act.wait_ge(q_parts, g)
                act.activation(qf[:, :], xb[0][:, :], ACT.Identity, bias=bias).then_inc(q_copied, 1)
                if free:
                    act.wait_ge(q_out, 16 * g)
                act.activation(qp[:, Q_SLOT[0], :], xb[0][:, :], ACT.Identity, bias=bias).then_inc(q_copied, 1)

            def exps(i, u, s):
                g = nr(i, u)
                act.wait_ge(st_mm, PAIRS * g + s + 1)
                act.activation(probs[:, ORDER[s], :], st[s % 2][:, :], ACT.Exp, scale=SCALE).then_inc(exp_done, 1)

            def copy_v(i, u):
                act.wait_ge(v_mm, nr(i, u) + 1)
                for hh in range(2):
                    rows = slice(hh * S, (hh + 1) * S)
                    src = xb[0][rows, :].rearrange("k (c q d) -> k c q d", q=2, d=DK)
                    for q in range(2):
                        col = q * 2 * DK + hh * DK
                        last = act.activation(Vs[u][rows, :, q::2, col:col + DK], src[:, :, q, :].rearrange(
                            "k (b j) d -> k b j d", b=GB), ACT.Copy)
                last.then_inc(v_done, 1)

            def copy_shift(i, u, free=True):
                g = nr(i, u)
                act.wait_ge(shift_mm, g + 1)
                if free:
                    act.wait_ge(shift_out, 16 * g)
                act.activation(shiftT[:, :, :].rearrange("c h (b q) -> c b h q", q=S),
                               xb[1][0:PARTS * PAIRS, :].bitcast(BF16).rearrange("c (b h q) -> c b h q", h=2, q=S),
                               ACT.Copy).then_inc(shift_copied, 1)
                act.wait_ge(shift_copied, g + 1)
                act.dma_start(shift_scratch.rearrange("h c n -> c h n"), shiftT[:]).then_inc(shift_out, 16)

            copy_k(0, 0, free=False)
            copy_xnT(0, 0)
            copy_q(0, 0, free=False)
            copy_k(0, 1)
            copy_xnT(0, 1)
            copy_q(0, 1)
            copy_shift(0, 0, free=False)
            act.wait_ge(vs_zero, 2)
            copy_v(0, 0)

            def step(i, u):
                one, two = after(i, u, 1), after(i, u, 2)
                exps(i, u, 0)
                if two:
                    copy_k(*two)
                exps(i, u, 1)
                if two:
                    copy_xnT(*two)
                exps(i, u, 2)
                exps(i, u, 3)
                if two:
                    copy_q(*two)
                exps(i, u, 4)
                exps(i, u, 5)
                exps(i, u, 6)
                exps(i, u, 7)
                if one:
                    copy_shift(*one)
                    copy_v(*one)

            with act.Fori(0, LOOPS) as i:
                step(i, 0)
                step(i, 1)
            for g in range(2 * LOOPS, G):
                step(g // 2, g % 2)
            act.wait_ge(keep_known, 1)
            go = act.value_load(any_keep_i[0:1, 0:1], min_val=0, max_val=1)
            with act.If(go > 0):
                act.wait_ge(ew_in, 64)
                with act.Fori(0, G) as g:
                    act.wait_ge(e_sub, g + 1)
                    act.activation(comb[:], ga[:, 0:NT, :], ACT.Exp).then_inc(e_exp, 1)
                    act.wait_ge(xeT_mm, g + 1)
                    act.activation(xeT[:, :], xb[1][:, :], ACT.Copy).then_inc(xeT_done, 1)
                    for e in range(E):
                        act.wait_ge(hid_mm, E * g + e + 1)
                        act.activation(hidden[e % 2][:, :], xb[0][:, :], ACT.Relu,
                                       bias=b1s[:, e:e + 1]).then_inc(hid_done, 1)

        @block.vector
        def _(dve):
            def row_stats(chain, stats, mv, var, rows):
                for t in range(NT):
                    ins = dve.bn_stats(stats[:, t, :], rows[:, t, 0:D])
                chain.link(ins)
                dve.memset(after_stats[:, :], 0.0)
                for t in range(NT):
                    ins = dve.bn_aggr(mv[:, t, :], stats[:, t, :])
                chain.link(ins)
                return dve.tensor_scalar(var[:, :], mv[:, :, 1], EPS, None, ALU.add)

            def ln1(i, u, free=True):
                g = nr(i, u)
                dve.wait_ge(x_in[u], 16 * (i + 1))
                if free:
                    dve.wait_ge(xn_done, g)
                c = Chain(dve, ln1_chain, 2 * g)
                row_stats(c, stats1, mv1, var1, xin[u]).then_inc(ln1_done, 1)

            def normalise(i, u, free=True):
                g = nr(i, u)
                if free:
                    dve.wait_ge(xnT_mm, g)
                dve.wait_ge(r1_done, g + 1)
                for t in range(NT):
                    last = dve.tensor_scalar(xn[:, t, :], xin[u][:, t, :], mv1[:, t, 0:1], r1[:, t:t + 1],
                                             ALU.subtract, ALU.mult)
                last.then_inc(xn_done, 1)

            def block_q(i, u, pairs):
                dve.wait_ge(q_in[u], Q_SPREAD * (i + 1))
                for hh in range(2):
                    last = dve.tensor_scalar(Qb[:, pairs, :, hh, :],
                                             Qs[u][0:ROWS, pairs, :].rearrange("r p (b q) -> r p b q", q=S),
                                             cst[0:ROWS, C_MASK + hh:C_MASK + hh + 1], None, ALU.mult)
                last.then_inc(q_blocks, 1)

            def block_k(i, u, hh):
                g = nr(i, u)
                if hh == 0:
                    dve.wait_ge(k_in[u], K_SPREAD * (i + 1))
                last = dve.tensor_scalar(Ks[u][0:ROWS, :, :, hh, :],
                                         Kn[u][:, :, :].rearrange("r p (b k) -> r p b k", k=S),
                                         cst[0:ROWS, C_MASK + hh:C_MASK + hh + 1], None, ALU.mult)
                if hh == 1:
                    last.then_inc(k_blocks, 1)

            def row_max(i, u, p):
                dve.wait_ge(s_mm, PAIRS * nr(i, u) + p + 1)
                dve.tensor_reduce(neg_max[:, :, p], sc[p % 2][:, :].rearrange("q (b k) -> q b k", k=S), AX.X, ALU.max,
                                  negate=True).then_inc(max_done, 1)

            def neg_part(n):
                return neg_parts[:, :, n * PAIRS:(n + 1) * PAIRS]

            def shift_parts(i, u, free=True):
                g = nr(i, u)
                dve.wait_ge(max_done, PAIRS * (g + 1))
                if free:
                    dve.wait_ge(shift_mm, g)
                c = Chain(dve, neg_chain, 2 * g)
                c.link(dve.tensor_copy(neg_part(0), neg_max[:]))
                dve.tensor_tensor(neg_rest[:], neg_max[:], neg_part(0), ALU.subtract)
                c.link(dve.tensor_tensor(neg_part(1), neg_max[:], neg_part(0), ALU.subtract))
                dve.tensor_tensor(neg_part(2), neg_rest[:], neg_part(1), ALU.subtract).then_inc(neg_done, 1)

            def quotients(i, u):
                g = nr(i, u)
                dve.wait_ge(den_mm, g + 1)
                c = Chain(dve, norm_chain, 2 * g)
                for n in range(2):
                    half = slice(n * GT // 2, (n + 1) * GT // 2)
                    c.link(dve.reciprocal(inv_den[:, half], den_ps[:, half]))
                    if n == 0:
                        dve.wait_ge(o_mm, g + 1)
                    dve.tensor_tensor(attnT[:, half], o_ps[:, half], inv_den[:, half], ALU.mult).then_inc(norm_done, 1)

            def residual(i, u):
                g = nr(i, u)
                dve.wait_ge(x1_free[u], 16 * (i + 1))
                for n in range(2):
                    dve.wait_ge(mix_mm, 2 * g + n + 1)
                    mixed = sc[n][:, 0:2 * DX].rearrange("p (t d) -> p t d", d=DX)
                    dve.tensor_tensor(logits[:, bass.ds(g * (NT * E) + 2 * n * E, 2 * E)].rearrange(
                        "p (t e) -> p t e", e=E), mixed[:, :, D:DX],
                        bias_row[:, D:DX].unsqueeze(1).to_broadcast([P, 2, E]), ALU.add)
                    dve.tensor_tensor(x1[u][:, 2 * n:2 * n + 2, :], mixed[:, :, 0:D],
                                      bias_row[:, 0:D].unsqueeze(1).to_broadcast([P, 2, D]),
                                      ALU.add).then_inc(x1_done, 1)

            def gates(groups, base):
                n = len(groups) * NT
                dve.wait_ge(x1_done, 2 * (groups[-1] + 2))
                c = Chain(dve, gate_chain, base)
                mine = slice(groups[0] * NT * E, (groups[-1] + 1) * NT * E)
                lo = logits[:, mine].rearrange("p (t e) -> p t e", e=E)
                pick(c, n, lo, top[:, 0, 0:n], top[:, 1, 0:n], first[:, 0:n, :])
                c.link(dve.scalar_tensor_tensor(out=gb[:, 0:n, :], in0=first[:, 0:n, :], scalar=-1e30, in1=lo,
                                                op0=ALU.mult, op1=ALU.add))
                pick(c, n, gb[:, 0:n, :], top[:, 2, 0:n], top[:, 3, 0:n], gc[:, 0:n, :])
                dve.tensor_tensor(picked[:, mine], first[:, 0:n, :].rearrange("p t e -> p (t e)"),
                                  gc[:, 0:n, :].rearrange("p t e -> p (t e)"), ALU.add).then_inc(gates_done, 1)
                return base + c.n

            def pick(c, n, src, best, lead, chosen):
                c.link(dve.tensor_reduce(best, src, AX.X, ALU.max))
                c.link(dve.tensor_tensor(chosen, src, wide(best, n), ALU.is_equal))
                c.link(dve.tensor_tensor(chosen, chosen, desc.unsqueeze(1).to_broadcast([P, n, E]), ALU.mult))
                c.link(dve.tensor_reduce(lead, chosen, AX.X, ALU.max))
                c.link(dve.tensor_tensor(chosen, chosen, wide(lead, n), ALU.is_equal))

            front, back = slice(0, HALF), slice(HALF, PAIRS)
            ln1(0, 0, free=False)
            dve.memset(neg_parts[:], 0.0).then_inc(neg_zero, 1)
            dve.memset(onesb[:], 1.0).then_inc(setup_dve, 1)
            dve.memset(one_row[:], 1.0).then_inc(setup_dve, 1)
            for u in range(2):
                dve.memset(x1[u][:, 0, 0:1], 0.0).then_inc(x1_free[u], 16)
                dve.memset(x1[u][:, 0, 1:2], 0.0).then_inc(x1_done, 1)
            normalise(0, 0, free=False)
            dve.wait_ge(w_in, 16)
            dve.tensor_copy(bv_wide[:], wts[:, W_BIAS + 2:W_BIAS + 3].to_broadcast([P, P])).then_inc(setup_dve, 1)
            dve.tensor_copy(bo_wide[:], wts[:, W_BIAS + 3:W_BIAS + 4].to_broadcast([P, P])).then_inc(setup_dve, 1)
            ln1(0, 1)
            dve.wait_ge(setup_pe, 1)
            dve.tensor_copy(cst[:, C_IDENT + P:C_IDENT + DX], st[0][:, 0:E]).then_inc(setup_dve, 1)
            dve.wait_ge(setup_pe, 2)
            dve.tensor_copy(wts[:, W_OT + D:W_OT + DX], st[1][:, 0:E]).then_inc(setup_dve, 1)
            normalise(0, 1)
            dve.wait_ge(setup_pe, 3)
            dve.tensor_copy(bias_row[:, :], st[0][:, 0:DX]).then_inc(setup_dve, 1)
            ln1(1, 0)
            dve.wait_ge(c_in, 32)
            block_k(0, 0, 0)
            block_k(0, 0, 1)
            block_q(0, 0, front)
            block_q(0, 0, back)
            for p in range(PAIRS):
                row_max(0, 0, p)
            dve.wait_ge(neg_zero, 1)
            shift_parts(0, 0, free=False)
            block_q(0, 1, front)
            block_q(0, 1, back)

            def step(i, u):
                one, two, three = (after(i, u, n) for n in range(1, 4))
                if one:
                    row_max(*one, 0)
                    row_max(*one, 1)
                if three:
                    ln1(*three)
                if one:
                    for p in range(2, PAIRS):
                        row_max(*one, p)
                    shift_parts(*one)
                    block_k(*one, 0)
                    block_k(*one, 1)
                quotients(i, u)
                residual(i, u)
                if two:
                    block_q(*two, front)
                    block_q(*two, back)

            with dve.Fori(0, LOOPS) as i:
                step(i, 0)
                step(i, 1)
            for g in range(2 * LOOPS, G - 1):
                step(g // 2, g % 2)
            links = gates(range(0, G - 1), 0)
            step((G - 1) // 2, (G - 1) % 2)
            gates(range(G - 1, G), links)

            dve.wait_ge(count_mm, 1)
            c = Chain(dve, count_chain, 0)
            c.link(dve.tensor_reduce(counts[:, :], st[0][:, 0:G * NT * E].rearrange("p (t e) -> p e t", e=E),
                                     AX.X, ALU.add))
            c.link(dve.tensor_scalar(keep[:, :], counts[:, :], float(CAP), None, ALU.is_le))
            c.link(dve.tensor_reduce(any_keep[:, :], keep[:, :], AX.X, ALU.max))
            dve.tensor_copy(any_keep_i[:, :], any_keep[:, :]).then_inc(keep_known, 1)
            dve.wait_ge(keep_known, 1)
            go = dve.value_load(any_keep_i[0:1, 0:1], min_val=0, max_val=1)
            with dve.If(go > 0):
                with dve.Fori(0, G) as g:
                    mine = bass.ds(g * (NT * E), NT * E)
                    c = Chain(dve, e_chain, 9 * g)
                    dve.wait_ge(xe_in, 16 * (g + 1))
                    row_stats(c, stats2, mv2, var2, xe).then_inc(var2_done, 1)
                    dve.wait_ge(r2_done, g + 1)
                    c.link(dve.tensor_tensor(gb[:, 0:NT, :], logits[:, mine].rearrange("p (t e) -> p t e", e=E),
                                             wide(r2[:, :]), ALU.mult))
                    c.link(dve.tensor_reduce(top[:, 0, 0:NT], gb[:, 0:NT, :], AX.X, ALU.max))
                    dve.tensor_tensor(ga[:, 0:NT, :], gb[:, 0:NT, :], wide(top[:, 0, 0:NT]),
                                      ALU.subtract).then_inc(e_sub, 1)
                    dve.wait_ge(e_exp, g + 1)
                    c.link(dve.tensor_reduce(esum[:, :], comb[:], AX.X, ALU.add))
                    c.link(dve.reciprocal(esum[:, :], esum[:, :]))
                    c.link(dve.tensor_tensor(comb[:], comb[:], wide(esum[:, :]), ALU.mult))
                    c.link(dve.tensor_tensor(comb[:], comb[:],
                                             picked[:, mine].rearrange("p (t e) -> p t e", e=E), ALU.mult))
                    c.link(dve.tensor_tensor(comb[:], comb[:],
                                             keep[:, :].unsqueeze(1).to_broadcast([P, NT, E]), ALU.mult))
                    assert c.n == 9
                    for t in range(NT):
                        ins = dve.tensor_scalar(xe_n[:, t, :], xe[:, t, :], mv2[:, t, 0:1], r2[:, t:t + 1],
                                                ALU.subtract, ALU.mult)
                    ins.then_inc(xe_done, 1)
                    dve.wait_ge(xe_done, g + 1)
                    for e in range(E):
                        dve.wait_ge(y_mm, E * g + e + 1)
                        if e:
                            dve.wait_ge(y_added, NT * E * g + NT * e)
                        for t in range(NT):
                            dve.scalar_tensor_tensor(out=xe[:, t, :], in0=st[e % 2][:, t * D:(t + 1) * D],
                                                     scalar=comb[:, t, e:e + 1], in1=xe[:, t, :],
                                                     op0=ALU.mult, op1=ALU.add).then_inc(y_added, 1)

        @block.tensor
        def _(pe):
            def k_proj(i, u):
                g = nr(i, u)
                pe.wait_ge(ctx_in[u], 16 * (i + 1))
                pe.matmul(xb[0][:, :], wts[:, W_K:W_K + D], ctxT[u][:, :], start=True, stop=True).then_inc(k_mm, 1)

            def transpose_xn(i, u):
                pe.wait_ge(xn_done, nr(i, u) + 1)
                for t in range(NT):
                    last = pe.transpose(xb[1][:, t * P:(t + 1) * P], xn[:, t, :], ident)
                last.then_inc(xnT_mm, 1)

            def q_proj(i, u):
                g = nr(i, u)
                pe.wait_ge(xnT_done, g + 1)
                pe.matmul(xb[0][:, :], wts[:, W_Q:W_Q + D], xnT[:, :], start=True, stop=True).then_inc(q_mm, 1)

            def v_proj(i, u):
                for b in range(GB):
                    for hh in range(2):
                        last = pe.matmul(xb[0][hh * S:(hh + 1) * S, b * 64:(b + 1) * 64],
                                         ctxT[u][:, b * S:(b + 1) * S], wts[:, W_V + hh * 64:W_V + (hh + 1) * 64],
                                         start=True, stop=True)
                last.then_inc(v_mm, 1)

            def scores(i, u, p):
                g = nr(i, u)
                if p == 0:
                    pe.wait_ge(k_in[u], K_SPREAD * (i + 1))
                if p % HALF == 0:
                    pe.wait_ge(q_blocks, 2 * g + p // HALF + 1)
                for b in range(GB):
                    last = pe.matmul(sc[p % 2][:, b * S:(b + 1) * S], Qb[:, p, b, :, :],
                                     Kn[u][:, p, b * S:(b + 1) * S], start=True, stop=True)
                last.then_inc(s_mm, 1)

            def transpose_shift(i, u):
                pe.wait_ge(neg_done, nr(i, u) + 1)
                dst = xb[1][0:SHIFT_COLS, :].bitcast(BF16)
                for b in range(GB):
                    last = pe.transpose(dst[:, b * P:(b + 1) * P], neg_parts[:, b, :], identb[:, :])
                last.then_inc(shift_mm, 1)

            def scores_t(i, u, s):
                g = nr(i, u)
                if s == 0:
                    pe.wait_ge(k_blocks, g + 1)
                    pe.wait_ge(shift_in, 16 * (g + 1))
                if s >= 2:
                    pe.wait_ge(exp_done, PAIRS * g + s - 1)
                p = ORDER[s]
                for b in range(GB):
                    cols = slice(b * S, (b + 1) * S)
                    last = pe.matmul(st[s % 2][:, cols], Ks[u][0:ROWS + SHIFT_ROWS, p, b, :, :],
                                     Qs[u][0:ROWS + SHIFT_ROWS, p, cols], start=True, stop=True)
                last.then_inc(st_mm, 1)

            def weigh(i, u, half, batches):
                g = nr(i, u)
                if batches[0] == 0:
                    pe.wait_ge(exp_done, PAIRS * g + HALF * (half + 1))
                    if half == 0:
                        pe.wait_ge(v_done, g + 1)
                for b in batches:
                    for s in range(half * HALF, (half + 1) * HALF):
                        p = ORDER[s]
                        j = p // 2
                        last = pe.matmul(o_ps[32 * j:32 * j + 32, b * S:(b + 1) * S], Vs[u][:, b, p, :],
                                  probs[:, p, b * S:(b + 1) * S], start=(half == 0 and b == 0),
                                  stop=(half == 1 and b == GB - 1), skip_group_check=True)
                if half == 1 and batches[-1] == GB - 1:
                    last.then_inc(o_mm, 1)

            def denominators(i, u, half):
                pe.wait_ge(exp_done, PAIRS * nr(i, u) + HALF * (half + 1))
                for s in range(half * HALF, (half + 1) * HALF):
                    p = ORDER[s]
                    j, q = p // 2, p % 2
                    last = pe.matmul(den_ps[32 * j:32 * j + 32, :], cst[:, C_ONES + 32 * q:C_ONES + 32 * q + 32],
                                     probs[:, p, :], start=(half == 0), stop=(half == 1), skip_group_check=True)
                    if s == HALF:
                        last.then_inc(qs_used, 1)
                if half == 1:
                    last.then_inc(den_mm, 1)

            def mix(i, u):
                g = nr(i, u)
                pe.wait_ge(xt_in[u], 16 * (i + 1))
                for t in range(NT):
                    if t % 2 == 0:
                        pe.wait_ge(norm_done, 2 * g + t // 2 + 1)
                    dst = sc[t // 2][:, (t % 2) * DX:(t % 2 + 1) * DX]
                    pe.matmul(dst, attnT[:, t * P:(t + 1) * P], rhs_attn, start=True, stop=False)
                    last = pe.matmul(dst, xT[u][:, t * P:(t + 1) * P], rhs_x, start=False, stop=True)
                    if t % 2:
                        last.then_inc(mix_mm, 1)

            pe.wait_ge(w_in, 16)
            k_proj(0, 0)
            pe.wait_ge(c_in, 32)
            pe.matmul(st[0][:, 0:E], cst[:, C_CENTRE:C_CENTRE + P], wts[:, W_G:W_G + E],
                      start=True, stop=True).then_inc(setup_pe, 1)
            transpose_xn(0, 0)
            pe.wait_ge(setup_dve, 5)
            pe.matmul(st[1][:, 0:E], wts[:, W_ON:W_ON + D], cst[:, C_IDENT + P:C_IDENT + DX],
                      start=True, stop=True).then_inc(setup_pe, 1)
            pe.wait_ge(k_copied, 2)
            q_proj(0, 0)
            pe.wait_ge(setup_dve, 6)
            pe.matmul(st[0][:, 0:DX], bv_wide[:, :], rhs_attn, start=True, stop=False).then_inc(qs_used, 1)
            pe.matmul(st[0][:, 0:DX], bo_wide[:, :], rhs_x, start=False, stop=True).then_inc(setup_pe, 1)
            transpose_xn(0, 1)
            pe.wait_ge(q_copied, 2)
            k_proj(0, 1)
            pe.wait_ge(k_copied, 4)
            q_proj(0, 1)
            for p in range(PAIRS):
                if p >= 2:
                    pe.wait_ge(max_done, p - 1)
                scores(0, 0, p)
            pe.wait_ge(xnT_done, 2)
            pe.wait_ge(c_in, 32)
            transpose_shift(0, 0)
            pe.wait_ge(q_copied, 4)
            v_proj(0, 0)
            pe.wait_ge(ones_in[0], 16)
            pe.wait_ge(ones_in[1], 16)
            pe.wait_ge(setup_dve, 7)

            def step(i, u):
                g = nr(i, u)
                one, two = after(i, u, 1), after(i, u, 2)
                near, far = range(GB // 2), range(GB // 2, GB)

                def next_scores(p):
                    if one is None:
                        return
                    if p == 0:
                        pe.wait_ge(x1_done, 2 * (g + 1))
                    elif p >= 2:
                        pe.wait_ge(max_done, PAIRS * (g + 1) + p - 1)
                    scores(*one, p)

                scores_t(i, u, 0)
                scores_t(i, u, 1)
                if two:
                    pe.wait_ge(v_done, g + 1)
                    k_proj(*two)
                if two:
                    pe.wait_ge(shift_copied, g + 1)
                    transpose_xn(*two)
                next_scores(0)
                scores_t(i, u, 2)
                next_scores(1)
                scores_t(i, u, 3)
                next_scores(2)
                if two:
                    pe.wait_ge(k_copied, 2 * (g + 3))
                    q_proj(*two)
                next_scores(3)
                weigh(i, u, 0, near)
                scores_t(i, u, 4)
                next_scores(4)
                weigh(i, u, 0, far)
                next_scores(5)
                scores_t(i, u, 5)
                next_scores(6)
                scores_t(i, u, 6)
                next_scores(7)
                denominators(i, u, 0)
                scores_t(i, u, 7)
                if one:
                    if two:
                        pe.wait_ge(xnT_done, g + 3)
                    transpose_shift(*one)
                denominators(i, u, 1)
                weigh(i, u, 1, near)
                weigh(i, u, 1, far)
                if one:
                    if two:
                        pe.wait_ge(q_copied, 2 * (g + 3))
                    v_proj(*one)
                    pe.wait_ge(max_done, PAIRS * (g + 2))
                mix(i, u)

            with pe.Fori(0, LOOPS) as i:
                step(i, 0)
                step(i, 1)
            for g in range(2 * LOOPS, G):
                step(g // 2, g % 2)
            pe.wait_ge(gates_done, 2)
            pe.matmul(st[0][:, 0:G * NT * E], onesb[:, :], picked[:, :], start=True, stop=True).then_inc(count_mm, 1)
            pe.wait_ge(keep_known, 1)
            go = pe.value_load(any_keep_i[0:1, 0:1], min_val=0, max_val=1)
            with pe.If(go > 0):
                pe.wait_ge(ew_in, 64)
                with pe.Fori(0, G) as g:
                    pe.wait_ge(xe_done, g + 1)
                    for t in range(NT):
                        ins = pe.transpose(xb[1][:, t * P:(t + 1) * P], xe_n[:, t, :], ident)
                    ins.then_inc(xeT_mm, 1)
                    pe.wait_ge(xeT_done, g + 1)

                    def hid(e):
                        if e:
                            pe.wait_ge(hid_done, E * g + e)
                        pe.matmul(xb[0][:, :], w1s[:, e, :], xeT[:, :], start=True, stop=True).then_inc(hid_mm, 1)

                    hid(0)
                    for e in range(E):
                        pe.wait_ge(hid_done, E * g + e + 1)
                        if e + 1 < E:
                            hid(e + 1)
                        if e >= 2:
                            pe.wait_ge(y_added, NT * E * g + NT * (e - 1))
                        for t in range(NT):
                            dst = st[e % 2][:, t * D:(t + 1) * D]
                            pe.matmul(dst, hidden[e % 2][:, t * P:(t + 1) * P], w2s[:, e, :], start=True, stop=False)
                            ins = pe.matmul(dst, one_row[:, :], b2s[:, e, :], start=False, stop=True)
                        ins.then_inc(y_mm, 1)


def kernel(**inputs):
    import ml_dtypes
    import numpy as np
    import concourse.bacc as bacc
    from concourse.bass_utils import run_bass_kernel_spmd

    a = {k: np.asarray(v) for k, v in inputs.items()}
    x = np.ascontiguousarray(a["x"].reshape(TOK, D))
    ctx = a["ctx_1024"].reshape(TOK, D)

    def by_group(m):
        return np.ascontiguousarray(m.reshape(G, GT, D).transpose(0, 2, 1))

    w = np.zeros((D, W_COLS), np.float32)
    order = np.arange(D).reshape(PAIRS, 2 * DK).T.reshape(D)
    w[:, W_Q:W_Q + D] = a["L0_xattn_Wq"].T[:, order]
    w[:, W_K:W_K + D] = a["L0_xattn_Wk"].T[:, order]
    w[:, W_V:W_V + D] = a["L0_xattn_Wv"].reshape(PAIRS, 2, DK, D).transpose(3, 1, 0, 2).reshape(D, D)
    w[:, W_OT:W_OT + D] = a["L0_xattn_Wo"].T
    w[:, W_ON:W_ON + D] = a["L0_xattn_Wo"]
    w[:, W_G:W_G + E] = a["L0_ffn_gate_w"].T
    for n, name in enumerate(("bq", "bk", "bv", "bo")):
        w[:, W_BIAS + n] = a["L0_xattn_" + name][order] if name in ("bq", "bk") else a["L0_xattn_" + name]
    c = np.zeros((P, C_COLS), np.float32)
    c[:, C_IDENT:C_IDENT + P] = np.eye(P)
    c[:, C_CENTRE:C_CENTRE + P] = np.eye(P) - 1.0 / D
    for q in range(2):
        for hh in range(2):
            first = C_ONES + 32 * q + 16 * q + 8 * hh
            c[hh * S:(hh + 1) * S, first:first + DK] = 1.0
    c[:, C_DESC:C_DESC + E] = np.arange(E, 0, -1)
    for hh in range(2):
        c[:ROWS, C_MASK + hh] = np.arange(ROWS) // DK % 2 == hh
    ones = np.zeros((SHIFT_ROWS, PAIRS, GB, 2, S), ml_dtypes.bfloat16)
    for hh in range(2):
        ones[hh * PARTS:(hh + 1) * PARTS, :, :, hh] = 1.0
    arrays = {
        "x_nat": x, "x_t": by_group(x), "ctx_t": by_group(ctx), "weights": w, "consts": c, "shift_ones": ones,
        "ident_b": np.eye(P).astype(ml_dtypes.bfloat16),
        "w1": np.ascontiguousarray(a["L0_ffn_W1"].transpose(1, 0, 2)),
        "w2": np.ascontiguousarray(a["L0_ffn_W2"].transpose(1, 0, 2)),
        "b1_t": np.ascontiguousarray(a["L0_ffn_b1"].T),
        "b2_rows": np.ascontiguousarray(a["L0_ffn_b2"].reshape(1, E, D)),
    }
    nc = bacc.Bacc("TRN2", target_bir_lowering=False, num_devices=1)
    aps = [nc.dram_tensor(n, v.shape, mybir.dt.from_np(v.dtype), kind="ExternalInput").ap()
           for n, v in arrays.items()]
    out = nc.dram_tensor("out", (TOK, D), F32, kind="ExternalOutput").ap()
    build(nc, *aps, out)
    r = run_bass_kernel_spmd(nc, [arrays], core_ids=[0])
    return r.results[0]["out"].reshape(B, S, D)
```

```python
from contextlib import ExitStack

import concourse.bass as bass
from concourse import mybir

F32 = mybir.dt.float32
BF16 = mybir.dt.bfloat16
I32 = mybir.dt.int32
ALU = mybir.AluOpType
ACT = mybir.ActivationFunctionType
AX = mybir.AxisListType

B, S, D = 64, 64, 128
H, DK = 16, 8
E = 8
TOK = B * S
P = 128
GT = 512
GB = GT // S
G = TOK // GT
NT = GT // P
PAIRS = H // 2
CAP = int(1.25 * TOK / E)
EPS = 1e-5
SCALE = DK ** -0.5
PARTS = 3
PRODUCTS = [(0, 0), (0, 1), (1, 0), (0, 2), (1, 1), (2, 0)]
Q_SLOT, K_SLOT = [0, 1, 2], [1, 0, 2]


def runs(slots):
    out = []
    for t, slot in enumerate(slots):
        if out and slot == out[-1][1] + out[-1][2]:
            out[-1] = (*out[-1][:2], out[-1][2] + 1)
        else:
            out.append((t, slot, 1))
    return out


Q_RUNS = runs([Q_SLOT[a] for a, _ in PRODUCTS])
K_RUNS = runs([K_SLOT[b] for _, b in PRODUCTS])
ROWS = len(PRODUCTS) * 2 * DK
SHIFT_ROWS = 2 * PARTS
DX = D + E
ORDER = [0, 2, 4, 6, 1, 3, 5, 7]
HALF = PAIRS // 2
GATE_TILES = (G - 1) * NT
Q_SPREAD, K_SPREAD = 16 * len(Q_RUNS), 16 * len(K_RUNS)
SHIFT_COLS = 32
W_Q, W_K, W_V, W_OT, W_ON = 0, D, 2 * D, 3 * D, 3 * D + DX
W_G = W_ON + D
W_BIAS = W_G + E
W_COLS = W_BIAS + 4
C_IDENT, C_CENTRE, C_ONES = 0, DX, DX + D
C_DESC = C_ONES + 64
C_MASK = C_DESC + E
C_COLS = C_MASK + 2


LOOPS = (G - 4) // 2


class Chain:

    def __init__(self, eng, sem, base):
        self.eng, self.sem, self.base, self.n = eng, sem, base, 0

    def link(self, ins):
        ins.then_inc(self.sem, 1)
        self.n += 1
        self.eng.wait_ge(self.sem, self.base + self.n)


def build(nc, x_nat, x_t, ctx_t, weights, consts, shift_ones, ident_b, w1, w2, b1_t, b2_rows, out):
    ctx = ExitStack()
    with ctx:
        def sb(name, shape, dt=F32):
            return ctx.enter_context(nc.sbuf_tensor(name, shape, dt))

        def ps(name):
            return ctx.enter_context(nc.psum_tensor(name, [P, 512], F32))

        def sem(name):
            return ctx.enter_context(nc.semaphore(name))

        wts = sb("wts", [P, W_COLS])
        cst = sb("cst", [P, C_COLS])
        identb = sb("identb", [P, P], BF16)
        onesb = sb("onesb", [P, P], BF16)
        bias_col = sb("bias_col", [P, 1])
        xin = [sb(f"xin{i}", [P, NT, D]) for i in range(2)]
        ctx_k = [sb(f"ctx_k{i}", [P, GT]) for i in range(2)]
        ctx_v = [sb(f"ctx_v{i}", [P, GT]) for i in range(2)]
        xT = [sb(f"xT{i}", [P, GT]) for i in range(2)]
        stats1 = sb("stats1", [P, NT, 6])
        after_stats = sb("after_stats", [P, 1])
        mv1 = sb("mv1", [P, NT, 2])
        var1 = sb("var1", [P, NT])
        r1 = sb("r1", [P, NT])
        power = sb("power", [P, NT])
        xn = sb("xn", [P, NT, D])
        xnT = sb("xnT", [P, GT])
        qf = sb("qf", [P, GT])
        kf = sb("kf", [P, GT])
        rest_q = sb("rest_q", [P, GT])
        rest_k = sb("rest_k", [P, GT])
        qp = sb("qp", [P, PARTS, GT], BF16)
        kp = sb("kp", [P, PARTS, GT], BF16)
        Qs = [sb(f"Qs{i}", [P, PAIRS, GT], BF16) for i in range(2)]
        Qb = sb("Qb", [ROWS, PAIRS, GB, 2, S], BF16)
        Kn = [sb(f"Kn{i}", [ROWS, PAIRS, GT], BF16) for i in range(2)]
        Ks = [sb(f"Ks{i}", [P, PAIRS, GB, 2, S], BF16) for i in range(2)]
        neg_max = sb("neg_max", [P, GB, PAIRS])
        neg_rest = sb("neg_rest", [P, GB, PAIRS])
        neg_parts = sb("neg_parts", [P, GB, SHIFT_COLS], BF16)
        shiftT = sb("shiftT", [PARTS * PAIRS, 2, GT], BF16)
        probs = sb("probs", [P, PAIRS, GT])
        Vs = [sb(f"Vs{i}", [P, GB, PAIRS, 32]) for i in range(2)]
        inv_den = sb("inv_den", [P, GT])
        attnT = sb("attnT", [P, GT])
        x1 = [sb(f"x1_{i}", [P, NT, D]) for i in range(2)]
        stats2 = sb("stats2", [P, NT, 6])
        mv2 = sb("mv2", [P, NT, 2])
        var2 = sb("var2", [P, NT])
        r2 = sb("r2", [P, NT])
        top = sb("top", [P, 4, GATE_TILES])
        ga = sb("ga", [P, GATE_TILES, E])
        gb = sb("gb", [P, GATE_TILES, E])
        first = sb("first", [P, GATE_TILES, E])
        gc = sb("gc", [P, GATE_TILES, E])
        logits = sb("logits", [P, G * NT * E])
        picked = sb("picked", [P, G * NT * E], BF16)
        counts = sb("counts", [P, E])
        keep = sb("keep", [P, E])
        any_keep = sb("any_keep", [P, 1])
        any_keep_i = sb("any_keep_i", [P, 1], I32)
        w1s = sb("w1s", [P, E, D])
        w2s = sb("w2s", [P, E, D])
        b1s = sb("b1s", [P, E])
        b2s = sb("b2s", [1, E, D])
        one_row = sb("one_row", [1, P])
        xe = sb("xe", [P, NT, D])
        xe_n = sb("xe_n", [P, NT, D])
        xeT = sb("xeT", [P, GT])
        hidden = [sb(f"hidden{i}", [P, GT]) for i in range(2)]
        comb = sb("comb", [P, NT, E])
        esum = sb("esum", [P, NT])

        st = [ps("st0"), ps("st1")]
        sc = [ps("sc0"), ps("sc1")]
        o_ps = ps("o_ps")
        den_ps = ps("den_ps")
        xb = [ps("xb0"), ps("xb1")]

        w_in = sem("w_in")
        c_in = sem("c_in")
        ones_in = [sem("ones_in0"), sem("ones_in1")]
        x_in = [sem("x_in0"), sem("x_in1")]
        ctx_k_in = [sem("ctx_k_in0"), sem("ctx_k_in1")]
        ctx_v_in = [sem("ctx_v_in0"), sem("ctx_v_in1")]
        xt_in = [sem("xt_in0"), sem("xt_in1")]
        q_in = [sem("q_in0"), sem("q_in1")]
        k_in = [sem("k_in0"), sem("k_in1")]
        q_blocks = sem("q_blocks")
        k_blocks = [sem("k_blocks0"), sem("k_blocks1")]
        shift_in = sem("shift_in")
        shift_out = sem("shift_out")
        k_out = sem("k_out")
        q_out = sem("q_out")
        x1_free = [sem("x1_free0"), sem("x1_free1")]
        setup_dve = sem("setup_dve")
        setup_pe = sem("setup_pe")
        vs_zero = sem("vs_zero")
        ln1_chain = sem("ln1_chain")
        ln1_done = sem("ln1_done")
        power_set = sem("power_set")
        r1_done = sem("r1_done")
        xt_biased = sem("xt_biased")
        xn_done = sem("xn_done")
        xnT_mm = sem("xnT_mm")
        xnT_done = sem("xnT_done")
        k_mm = sem("k_mm")
        k_copied = sem("k_copied")
        q_mm = sem("q_mm")
        q_copied = sem("q_copied")
        k_chain = sem("k_chain")
        q_chain = sem("q_chain")
        k_parts = sem("k_parts")
        q_parts = sem("q_parts")
        v_mm = sem("v_mm")
        v_done = sem("v_done")
        s_mm = sem("s_mm")
        max_done = sem("max_done")
        neg_chain = sem("neg_chain")
        neg_zero = sem("neg_zero")
        neg_done = sem("neg_done")
        shift_mm = sem("shift_mm")
        shift_copied = sem("shift_copied")
        st_mm = sem("st_mm")
        qs_used = sem("qs_used")
        exp_done = sem("exp_done")
        den_mm = sem("den_mm")
        o_mm = sem("o_mm")
        norm_chain = sem("norm_chain")
        norm_done = sem("norm_done")
        mix_mm = sem("mix_mm")
        x1_done = sem("x1_done")
        gate_chain = sem("gate_chain")
        gates_done = sem("gates_done")
        count_mm = sem("count_mm")
        count_chain = sem("count_chain")
        keep_known = sem("keep_known")
        ew_in = sem("ew_in")
        xe_in = sem("xe_in")
        e_chain = sem("e_chain")
        var2_done = sem("var2_done")
        r2_done = sem("r2_done")
        xe_done = sem("xe_done")
        xeT_mm = sem("xeT_mm")
        xeT_done = sem("xeT_done")
        hid_mm = sem("hid_mm")
        hid_done = sem("hid_done")
        y_mm = sem("y_mm")
        y_added = sem("y_added")
        e_exp = sem("e_exp")
        e_sub = sem("e_sub")
        e_stored = sem("e_stored")

        ident = cst[:, C_IDENT:C_IDENT + P]
        rhs_x = cst[:, C_IDENT:C_IDENT + DX]
        rhs_attn = wts[:, W_OT:W_OT + DX]
        desc = cst[:, C_DESC:C_DESC + E]
        x_dram = x_nat.rearrange("(g t p) d -> g p t d", t=NT, p=P)
        out_dram = out.rearrange("(g t p) d -> g p t d", t=NT, p=P)

        def wide(col, tiles=NT):
            return col.unsqueeze(2).to_broadcast([P, tiles, E])

        q_scratch, k_scratch = ([nc.dram_tensor(f"{n}_scratch{i}", (PARTS, P, GT), BF16, kind="Internal").ap()
                                 for i in range(2)] for n in "qk")
        q_rows = [s.rearrange("c (r p) n -> (c r) p n", p=PAIRS) for s in q_scratch]
        k_rows = [s.rearrange("c (r p) n -> (c r) p n", p=PAIRS) for s in k_scratch]
        shift_scratch = nc.dram_tensor("shift_scratch", (2, PARTS * PAIRS, GT), BF16, kind="Internal").ap()

        block = ctx.enter_context(nc.Block())

        def nr(i, u):
            return i * 2 + u

        def after(i, u, n):
            i, u = i + (u + n) // 2, (u + n) % 2
            return (i, u) if not isinstance(i, int) or nr(i, u) < G else None

        def parts(eng, i, u, copied, full, rest, pieces, slot, chain_sem, done):
            g = nr(i, u)
            eng.wait_ge(copied, 2 * (g + 1))
            c = Chain(eng, chain_sem, g)
            part = [pieces[:, slot[n], :] for n in range(PARTS)]
            eng.tensor_tensor(rest[:, :], full[:, :], part[0], ALU.subtract)
            c.link(eng.tensor_tensor(part[1], full[:, :], part[0], ALU.subtract))
            eng.tensor_tensor(part[2], rest[:, :], part[1], ALU.subtract).then_inc(done, 1)

        def write_k(eng, i, u):
            eng.wait_ge(k_parts, nr(i, u) + 1)
            eng.dma_start(k_scratch[u].rearrange("c f n -> f c n"), kp[:]).then_inc(k_out, 16)

        @block.sync
        def _(sp):
            def load_x(i, u, free=True):
                g = nr(i, u)
                if free:
                    sp.wait_ge(xn_done, g - 1)
                sp.dma_start(xin[u][:], x_dram[g]).then_inc(x_in[u], 16)

            def load_ctx_k(i, u, free=True):
                g = nr(i, u)
                if free:
                    sp.wait_ge(k_mm, g - 1)
                sp.dma_start(ctx_k[u][:], ctx_t[g]).then_inc(ctx_k_in[u], 16)

            def load_ctx_v(i, u, free=True):
                g = nr(i, u)
                if free:
                    sp.wait_ge(v_mm, g - 1)
                sp.dma_start(ctx_v[u][:], ctx_t[g]).then_inc(ctx_v_in[u], 16)

            def load_xt(i, u, free=True):
                g = nr(i, u)
                if free:
                    sp.wait_ge(mix_mm, 2 * (g - 1))
                sp.dma_start(xT[u][:], x_t[g]).then_inc(xt_in[u], 16)

            def write_q(i, u):
                sp.wait_ge(q_parts, nr(i, u) + 1)
                sp.dma_start(q_scratch[u].rearrange("c f n -> f c n"), qp[:]).then_inc(q_out, 16)

            def read_q(i, u, free=True):
                g = nr(i, u)
                sp.wait_ge(q_out, 16 * (g + 1))
                if free:
                    sp.wait_ge(qs_used, g)
                spread(Qs[u], q_rows[u], Q_RUNS, q_in[u])

            def spread(dst, rows, runs_of, done):
                for t, slot, n in runs_of:
                    sp.dma_start(dst[2 * t * DK:2 * (t + n) * DK, :, :],
                                 rows[2 * slot * DK:2 * (slot + n) * DK]).then_inc(done, 16)

            def read_k(i, u):
                g = nr(i, u)
                sp.wait_ge(k_out, 16 * (g + 1))
                sp.wait_ge(k_blocks[0], g + 1)
                spread(Kn[u], k_rows[u], K_RUNS, k_in[u])

            def read_shift(i, u):
                sp.wait_ge(shift_out, 16 * (nr(i, u) + 1))
                sp.dma_start(Qs[u][ROWS:ROWS + SHIFT_ROWS, :, :],
                             shift_scratch.rearrange("h (c p) n -> (h c) p n", p=PAIRS)).then_inc(shift_in, 16)

            def store(i, u):
                g = nr(i, u)
                sp.wait_ge(x1_done, 2 * (g + 2))
                sp.dma_start(out_dram[g], x1[u][:]).then_inc(x1_free[u], 16)

            sp.dma_start(xin[0][:], x_dram[0]).then_inc(x_in[0], 16)
            load_ctx_k(0, 0, free=False)
            sp.dma_start(wts[:], weights).then_inc(w_in, 16)
            sp.dma_start(cst[:], consts).then_inc(c_in, 16)
            load_x(0, 1, free=False)
            load_ctx_k(0, 1, free=False)
            sp.dma_start(identb[:], ident_b).then_inc(c_in, 16)
            for u in range(2):
                load_ctx_v(0, u, free=False)
                sp.dma_start(Ks[u][ROWS:ROWS + SHIFT_ROWS, :, :, :, :], shift_ones).then_inc(ones_in[u], 16)
                load_xt(0, u, free=False)
            load_x(1, 0)
            write_k(sp, 0, 0)
            write_q(0, 0)
            read_k(0, 0)
            read_q(0, 0, free=False)
            load_x(1, 1)
            load_ctx_k(1, 0)
            write_q(0, 1)
            write_k(sp, 0, 1)
            read_q(0, 1, free=False)
            read_k(0, 1)
            load_ctx_k(1, 1)
            read_shift(0, 0)
            write_k(sp, 1, 0)
            read_k(1, 0)

            def step(i, u):
                one, two, three, four = (after(i, u, n) for n in range(1, 5))
                if two:
                    write_q(*two)
                    read_q(*two)
                if one:
                    read_shift(*one)
                if four:
                    load_x(*four)
                    load_ctx_k(*four)
                if two:
                    load_ctx_v(*two)
                store(i, u)
                if two:
                    load_xt(*two)
                if three:
                    write_k(sp, *three)
                    read_k(*three)

            with sp.Fori(0, LOOPS) as i:
                step(i, 0)
                step(i, 1)
            for g in range(2 * LOOPS, G):
                step(g // 2, g % 2)
            for u in range(2):
                sp.wait_ge(x1_free[u], 16 * (G // 2 + 1))
            sp.wait_ge(keep_known, 1)
            go = sp.value_load(any_keep_i[0:1, 0:1], min_val=0, max_val=1)
            with sp.If(go > 0):
                for dst, src in ((w1s[:], w1), (w2s[:], w2), (b1s[:], b1_t), (b2s[:], b2_rows)):
                    sp.dma_start(dst, src).then_inc(ew_in, 16)
                sp.dma_start(xe[:], out_dram[0]).then_inc(xe_in, 16)
                with sp.Fori(0, G - 1) as g:
                    sp.wait_ge(y_added, NT * E * (g + 1))
                    sp.dma_start(out_dram[g], xe[:]).then_inc(e_stored, 16)
                    sp.wait_ge(e_stored, 16 * (g + 1))
                    sp.dma_start(xe[:], out_dram[g + 1]).then_inc(xe_in, 16)
                sp.wait_ge(y_added, NT * E * G)
                sp.dma_start(out_dram[G - 1], xe[:]).then_inc(e_stored, 16)
                sp.wait_ge(e_stored, 16 * G)

        @block.gpsimd
        def _(pool):
            def inverse_root1(i, u, free=True):
                g = nr(i, u)
                pool.wait_ge(ln1_done, g + 1)
                if free:
                    pool.wait_ge(xnT_mm, g)
                inverse_root(var1, r1, r1_done)

            def normalise(i, u):
                pool.wait_ge(power_set, 1)
                pool.wait_ge(r1_done, nr(i, u) + 1)
                for t in range(NT):
                    last = pool.tensor_scalar(xn[:, t, :], xin[u][:, t, :], mv1[:, t, 0:1], r1[:, t:t + 1],
                                              ALU.subtract, ALU.mult)
                last.then_inc(xn_done, 1)

            def inverse_root(var, r, done):
                pool.tensor_tensor(r[:, :], var[:, :], power[:, :], ALU.pow).then_inc(done, 1)

            def bias_x(i, u):
                pool.wait_ge(xt_in[u], 16 * (i + 1))
                pool.tensor_tensor(xT[u][:, :], xT[u][:, :], bias_col[:, :].to_broadcast([P, GT]),
                                   ALU.add).then_inc(xt_biased, 1)

            def parts_k(i, u):
                parts(pool, i, u, k_copied, kf, rest_k, kp, K_SLOT, k_chain, k_parts)

            def parts_q(i, u):
                parts(pool, i, u, q_copied, qf, rest_q, qp, Q_SLOT, q_chain, q_parts)

            pool.memset(power[:, :], -0.5).then_inc(power_set, 1)
            pool.wait_ge(power_set, 1)
            inverse_root1(0, 0, free=False)
            parts_k(0, 0)
            inverse_root1(0, 1)
            for u in range(2):
                pool.memset(Vs[u][:], 0.0).then_inc(vs_zero, 1)
            parts_q(0, 1)
            parts_k(0, 1)
            inverse_root1(1, 0)
            pool.wait_ge(setup_dve, 5)
            bias_x(0, 0)
            normalise(1, 0)
            parts_k(1, 0)

            def step(i, u):
                one, two, three = (after(i, u, n) for n in range(1, 4))
                if two:
                    parts_q(*two)
                if three:
                    inverse_root1(*three)
                    normalise(*three)
                    parts_k(*three)
                if one:
                    bias_x(*one)

            with pool.Fori(0, LOOPS) as i:
                step(i, 0)
                step(i, 1)
            for g in range(2 * LOOPS, G):
                step(g // 2, g % 2)
            pool.wait_ge(keep_known, 1)
            go = pool.value_load(any_keep_i[0:1, 0:1], min_val=0, max_val=1)
            with pool.If(go > 0):
                with pool.Fori(0, G) as g:
                    pool.wait_ge(var2_done, g + 1)
                    inverse_root(var2, r2, r2_done)

        @block.scalar
        def _(act):
            def copy_xnT(i, u):
                act.wait_ge(xnT_mm, nr(i, u) + 1)
                act.activation(xnT[:, :], xb[1][:, :], ACT.Copy).then_inc(xnT_done, 1)

            def copy_k(i, u, free=True):
                g = nr(i, u)
                act.wait_ge(k_mm, g + 1)
                bias = wts[:, W_BIAS + 1:W_BIAS + 2]
                if free:
                    act.wait_ge(k_parts, g)
                act.activation(kf[:, :], xb[0][:, :], ACT.Identity, bias=bias).then_inc(k_copied, 1)
                if free:
                    act.wait_ge(k_out, 16 * g)
                act.activation(kp[:, K_SLOT[0], :], xb[0][:, :], ACT.Identity, bias=bias).then_inc(k_copied, 1)

            def copy_q(i, u, free=True):
                g = nr(i, u)
                act.wait_ge(q_mm, g + 1)
                bias = wts[:, W_BIAS:W_BIAS + 1]
                if free:
                    act.wait_ge(q_parts, g)
                act.activation(qf[:, :], xb[0][:, :], ACT.Identity, bias=bias).then_inc(q_copied, 1)
                if free:
                    act.wait_ge(q_out, 16 * g)
                act.activation(qp[:, Q_SLOT[0], :], xb[0][:, :], ACT.Identity, bias=bias).then_inc(q_copied, 1)

            def exps(i, u, s):
                g = nr(i, u)
                act.wait_ge(st_mm, PAIRS * g + s + 1)
                act.activation(probs[:, ORDER[s], :], st[s % 2][:, :], ACT.Exp, scale=SCALE).then_inc(exp_done, 1)

            def copy_v(i, u):
                act.wait_ge(v_mm, nr(i, u) + 1)
                for hh in range(2):
                    rows = slice(hh * S, (hh + 1) * S)
                    src = xb[0][rows, :].rearrange("k (c q d) -> k c q d", q=2, d=DK)
                    for q in range(2):
                        col = q * 2 * DK + hh * DK
                        last = act.activation(Vs[u][rows, :, q::2, col:col + DK], src[:, :, q, :].rearrange(
                            "k (b j) d -> k b j d", b=GB), ACT.Copy)
                last.then_inc(v_done, 1)

            def block_k(i, u):
                act.wait_ge(k_in[u], K_SPREAD * (i + 1))
                act.activation(Ks[u][0:ROWS, :, :, 1, :], Kn[u][:, :, :].rearrange("r p (b k) -> r p b k", k=S),
                               ACT.Copy, scale=cst[0:ROWS, C_MASK + 1:C_MASK + 2]).then_inc(k_blocks[1], 1)

            def residual(i, u):
                g = nr(i, u)
                act.wait_ge(x1_free[u], 16 * (i + 1))
                for n in range(2):
                    act.wait_ge(mix_mm, 2 * g + n + 1)
                    mixed = sc[n][:, 0:2 * DX].rearrange("p (t d) -> p t d", d=DX)
                    act.activation(logits[:, bass.ds(g * (NT * E) + 2 * n * E, 2 * E)].rearrange(
                        "p (t e) -> p t e", e=E), mixed[:, :, D:DX], ACT.Copy)
                    act.activation(x1[u][:, 2 * n:2 * n + 2, :], mixed[:, :, 0:D], ACT.Copy).then_inc(x1_done, 1)

            def copy_shift(i, u, free=True):
                g = nr(i, u)
                act.wait_ge(shift_mm, g + 1)
                if free:
                    act.wait_ge(shift_out, 16 * g)
                act.activation(shiftT[:, :, :].rearrange("c h (b q) -> c b h q", q=S),
                               xb[1][0:PARTS * PAIRS, :].bitcast(BF16).rearrange("c (b h q) -> c b h q", h=2, q=S),
                               ACT.Copy).then_inc(shift_copied, 1)
                act.wait_ge(shift_copied, g + 1)
                act.dma_start(shift_scratch.rearrange("h c n -> c h n"), shiftT[:]).then_inc(shift_out, 16)

            copy_k(0, 0, free=False)
            copy_xnT(0, 0)
            copy_q(0, 0, free=False)
            copy_xnT(0, 1)
            copy_q(0, 1)
            copy_k(0, 1)
            act.wait_ge(c_in, 32)
            block_k(0, 0)
            copy_k(1, 0)
            copy_shift(0, 0, free=False)
            act.wait_ge(vs_zero, 2)
            copy_v(0, 0)
            copy_xnT(1, 0)

            def step(i, u):
                one, two, three = (after(i, u, n) for n in range(1, 4))
                exps(i, u, 0)
                exps(i, u, 1)
                if two:
                    copy_q(*two)
                exps(i, u, 2)
                for s in range(3, PAIRS):
                    exps(i, u, s)
                if one:
                    copy_shift(*one)
                if three:
                    copy_k(*three)
                if one:
                    block_k(*one)
                    copy_v(*one)
                residual(i, u)
                if three:
                    copy_xnT(*three)

            with act.Fori(0, LOOPS) as i:
                step(i, 0)
                step(i, 1)
            for g in range(2 * LOOPS, G):
                step(g // 2, g % 2)
            act.wait_ge(keep_known, 1)
            go = act.value_load(any_keep_i[0:1, 0:1], min_val=0, max_val=1)
            with act.If(go > 0):
                act.wait_ge(ew_in, 64)
                with act.Fori(0, G) as g:
                    act.wait_ge(e_sub, g + 1)
                    act.activation(comb[:], ga[:, 0:NT, :], ACT.Exp).then_inc(e_exp, 1)
                    act.wait_ge(xeT_mm, g + 1)
                    act.activation(xeT[:, :], xb[1][:, :], ACT.Copy).then_inc(xeT_done, 1)
                    for e in range(E):
                        act.wait_ge(hid_mm, E * g + e + 1)
                        act.activation(hidden[e % 2][:, :], xb[0][:, :], ACT.Relu,
                                       bias=b1s[:, e:e + 1]).then_inc(hid_done, 1)

        @block.vector
        def _(dve):
            def row_stats(chain, stats, mv, var, rows):
                for t in range(NT):
                    ins = dve.bn_stats(stats[:, t, :], rows[:, t, 0:D])
                chain.link(ins)
                dve.memset(after_stats[:, :], 0.0)
                for t in range(NT):
                    ins = dve.bn_aggr(mv[:, t, :], stats[:, t, :])
                chain.link(ins)
                return dve.tensor_scalar(var[:, :], mv[:, :, 1], EPS, None, ALU.add)

            def ln1(i, u, free=True):
                g = nr(i, u)
                dve.wait_ge(x_in[u], 16 * (i + 1))
                if free:
                    dve.wait_ge(xn_done, g)
                c = Chain(dve, ln1_chain, 2 * g)
                row_stats(c, stats1, mv1, var1, xin[u]).then_inc(ln1_done, 1)

            def normalise(i, u, free=True):
                g = nr(i, u)
                if free:
                    dve.wait_ge(xnT_mm, g)
                dve.wait_ge(r1_done, g + 1)
                for t in range(NT):
                    last = dve.tensor_scalar(xn[:, t, :], xin[u][:, t, :], mv1[:, t, 0:1], r1[:, t:t + 1],
                                             ALU.subtract, ALU.mult)
                last.then_inc(xn_done, 1)

            def block_q(i, u, pairs):
                dve.wait_ge(q_in[u], Q_SPREAD * (i + 1))
                for hh in range(2):
                    last = dve.tensor_scalar(Qb[:, pairs, :, hh, :],
                                             Qs[u][0:ROWS, pairs, :].rearrange("r p (b q) -> r p b q", q=S),
                                             cst[0:ROWS, C_MASK + hh:C_MASK + hh + 1], None, ALU.mult)
                last.then_inc(q_blocks, 1)

            def block_k(i, u):
                dve.wait_ge(k_in[u], K_SPREAD * (i + 1))
                dve.tensor_scalar(Ks[u][0:ROWS, :, :, 0, :], Kn[u][:, :, :].rearrange("r p (b k) -> r p b k", k=S),
                                  cst[0:ROWS, C_MASK:C_MASK + 1], None, ALU.mult).then_inc(k_blocks[0], 1)

            def row_max(i, u, p):
                dve.wait_ge(s_mm, PAIRS * nr(i, u) + p + 1)
                dve.tensor_reduce(neg_max[:, :, p], sc[p % 2][:, :].rearrange("q (b k) -> q b k", k=S), AX.X, ALU.max,
                                  negate=True).then_inc(max_done, 1)

            def neg_part(n):
                return neg_parts[:, :, n * PAIRS:(n + 1) * PAIRS]

            def shift_parts(i, u, free=True):
                g = nr(i, u)
                dve.wait_ge(max_done, PAIRS * (g + 1))
                if free:
                    dve.wait_ge(shift_mm, g)
                c = Chain(dve, neg_chain, 2 * g)
                c.link(dve.tensor_copy(neg_part(0), neg_max[:]))
                dve.tensor_tensor(neg_rest[:], neg_max[:], neg_part(0), ALU.subtract)
                c.link(dve.tensor_tensor(neg_part(1), neg_max[:], neg_part(0), ALU.subtract))
                dve.tensor_tensor(neg_part(2), neg_rest[:], neg_part(1), ALU.subtract).then_inc(neg_done, 1)

            def quotients(i, u):
                g = nr(i, u)
                dve.wait_ge(den_mm, g + 1)
                c = Chain(dve, norm_chain, 2 * g)
                halves = [slice(n * GT // 2, (n + 1) * GT // 2) for n in range(2)]
                for half in halves:
                    c.link(dve.reciprocal(inv_den[:, half], den_ps[:, half]))
                dve.wait_ge(o_mm, g + 1)
                for half in halves:
                    dve.tensor_tensor(attnT[:, half], o_ps[:, half], inv_den[:, half], ALU.mult).then_inc(norm_done, 1)

            def gates(groups, base):
                n = len(groups) * NT
                dve.wait_ge(x1_done, 2 * (groups[-1] + 2))
                c = Chain(dve, gate_chain, base)
                mine = slice(groups[0] * NT * E, (groups[-1] + 1) * NT * E)
                lo = logits[:, mine].rearrange("p (t e) -> p t e", e=E)
                pick(c, n, lo, top[:, 0, 0:n], top[:, 1, 0:n], first[:, 0:n, :])
                c.link(dve.scalar_tensor_tensor(out=gb[:, 0:n, :], in0=first[:, 0:n, :], scalar=-1e30, in1=lo,
                                                op0=ALU.mult, op1=ALU.add))
                pick(c, n, gb[:, 0:n, :], top[:, 2, 0:n], top[:, 3, 0:n], gc[:, 0:n, :])
                dve.tensor_tensor(picked[:, mine], first[:, 0:n, :].rearrange("p t e -> p (t e)"),
                                  gc[:, 0:n, :].rearrange("p t e -> p (t e)"), ALU.add).then_inc(gates_done, 1)
                return base + c.n

            def pick(c, n, src, best, lead, chosen):
                c.link(dve.tensor_reduce(best, src, AX.X, ALU.max))
                c.link(dve.tensor_tensor(chosen, src, wide(best, n), ALU.is_equal))
                c.link(dve.tensor_tensor(chosen, chosen, desc.unsqueeze(1).to_broadcast([P, n, E]), ALU.mult))
                c.link(dve.tensor_reduce(lead, chosen, AX.X, ALU.max))
                c.link(dve.tensor_tensor(chosen, chosen, wide(lead, n), ALU.is_equal))

            front, back = slice(0, HALF), slice(HALF, PAIRS)
            ln1(0, 0, free=False)
            dve.memset(neg_parts[:], 0.0).then_inc(neg_zero, 1)
            dve.memset(onesb[:], 1.0).then_inc(setup_dve, 1)
            dve.memset(one_row[:], 1.0).then_inc(setup_dve, 1)
            for u in range(2):
                dve.memset(Kn[u][:, 0, 0:1], 0.0).then_inc(k_blocks[0], 1)
                dve.memset(x1[u][:, 0, 0:1], 0.0).then_inc(x1_free[u], 16)
                dve.memset(x1[u][:, 0, 1:2], 0.0).then_inc(x1_done, 1)
            normalise(0, 0, free=False)
            ln1(0, 1)
            dve.wait_ge(setup_pe, 1)
            dve.tensor_copy(cst[:, C_IDENT + P:C_IDENT + DX], st[0][:, 0:E]).then_inc(setup_dve, 1)
            dve.wait_ge(setup_pe, 2)
            dve.tensor_copy(wts[:, W_OT + D:W_OT + DX], st[1][:, 0:E]).then_inc(setup_dve, 1)
            parts(dve, 0, 0, q_copied, qf, rest_q, qp, Q_SLOT, q_chain, q_parts)
            normalise(0, 1)
            ln1(1, 0)
            dve.wait_ge(setup_pe, 3)
            dve.wait_ge(w_in, 16)
            dve.tensor_tensor(bias_col[:, :], st[0][:, 0:1], wts[:, W_BIAS + 3:W_BIAS + 4], ALU.add).then_inc(setup_dve, 1)
            dve.wait_ge(c_in, 32)
            block_k(0, 0)
            block_q(0, 0, front)
            block_q(0, 0, back)
            for p in range(PAIRS):
                row_max(0, 0, p)
            dve.wait_ge(neg_zero, 1)
            shift_parts(0, 0, free=False)
            block_q(0, 1, front)
            block_q(0, 1, back)

            def step(i, u):
                one, two, three = (after(i, u, n) for n in range(1, 4))
                if one:
                    for p in range(PAIRS):
                        row_max(*one, p)
                    shift_parts(*one)
                if three:
                    ln1(*three)
                quotients(i, u)
                if one:
                    block_k(*one)
                if two:
                    block_q(*two, front)
                    block_q(*two, back)

            with dve.Fori(0, LOOPS) as i:
                step(i, 0)
                step(i, 1)
            for g in range(2 * LOOPS, G - 1):
                step(g // 2, g % 2)
            links = gates(range(0, G - 1), 0)
            step((G - 1) // 2, (G - 1) % 2)
            gates(range(G - 1, G), links)

            dve.wait_ge(count_mm, 1)
            c = Chain(dve, count_chain, 0)
            c.link(dve.tensor_reduce(counts[:, :], st[0][:, 0:G * NT * E].rearrange("p (t e) -> p e t", e=E),
                                     AX.X, ALU.add))
            c.link(dve.tensor_scalar(keep[:, :], counts[:, :], float(CAP), None, ALU.is_le))
            c.link(dve.tensor_reduce(any_keep[:, :], keep[:, :], AX.X, ALU.max))
            dve.tensor_copy(any_keep_i[:, :], any_keep[:, :]).then_inc(keep_known, 1)
            dve.wait_ge(keep_known, 1)
            go = dve.value_load(any_keep_i[0:1, 0:1], min_val=0, max_val=1)
            with dve.If(go > 0):
                with dve.Fori(0, G) as g:
                    mine = bass.ds(g * (NT * E), NT * E)
                    c = Chain(dve, e_chain, 9 * g)
                    dve.wait_ge(xe_in, 16 * (g + 1))
                    row_stats(c, stats2, mv2, var2, xe).then_inc(var2_done, 1)
                    dve.wait_ge(r2_done, g + 1)
                    c.link(dve.tensor_tensor(gb[:, 0:NT, :], logits[:, mine].rearrange("p (t e) -> p t e", e=E),
                                             wide(r2[:, :]), ALU.mult))
                    c.link(dve.tensor_reduce(top[:, 0, 0:NT], gb[:, 0:NT, :], AX.X, ALU.max))
                    dve.tensor_tensor(ga[:, 0:NT, :], gb[:, 0:NT, :], wide(top[:, 0, 0:NT]),
                                      ALU.subtract).then_inc(e_sub, 1)
                    dve.wait_ge(e_exp, g + 1)
                    c.link(dve.tensor_reduce(esum[:, :], comb[:], AX.X, ALU.add))
                    c.link(dve.reciprocal(esum[:, :], esum[:, :]))
                    c.link(dve.tensor_tensor(comb[:], comb[:], wide(esum[:, :]), ALU.mult))
                    c.link(dve.tensor_tensor(comb[:], comb[:],
                                             picked[:, mine].rearrange("p (t e) -> p t e", e=E), ALU.mult))
                    c.link(dve.tensor_tensor(comb[:], comb[:],
                                             keep[:, :].unsqueeze(1).to_broadcast([P, NT, E]), ALU.mult))
                    assert c.n == 9
                    for t in range(NT):
                        ins = dve.tensor_scalar(xe_n[:, t, :], xe[:, t, :], mv2[:, t, 0:1], r2[:, t:t + 1],
                                                ALU.subtract, ALU.mult)
                    ins.then_inc(xe_done, 1)
                    dve.wait_ge(xe_done, g + 1)
                    for e in range(E):
                        dve.wait_ge(y_mm, E * g + e + 1)
                        if e:
                            dve.wait_ge(y_added, NT * E * g + NT * e)
                        for t in range(NT):
                            dve.scalar_tensor_tensor(out=xe[:, t, :], in0=st[e % 2][:, t * D:(t + 1) * D],
                                                     scalar=comb[:, t, e:e + 1], in1=xe[:, t, :],
                                                     op0=ALU.mult, op1=ALU.add).then_inc(y_added, 1)

        @block.tensor
        def _(pe):
            def k_proj(i, u):
                g = nr(i, u)
                pe.wait_ge(ctx_k_in[u], 16 * (i + 1))
                pe.matmul(xb[0][:, :], wts[:, W_K:W_K + D], ctx_k[u][:, :], start=True, stop=True).then_inc(k_mm, 1)

            def transpose_xn(i, u):
                pe.wait_ge(xn_done, nr(i, u) + 1)
                for t in range(NT):
                    last = pe.transpose(xb[1][:, t * P:(t + 1) * P], xn[:, t, :], ident)
                last.then_inc(xnT_mm, 1)

            def q_proj(i, u):
                pe.wait_ge(xnT_done, nr(i, u) + 1)
                pe.matmul(xb[0][:, :], wts[:, W_Q:W_Q + D], xnT[:, :], start=True, stop=True).then_inc(q_mm, 1)

            def v_proj(i, u):
                pe.wait_ge(ctx_v_in[u], 16 * (i + 1))
                for b in range(GB):
                    for hh in range(2):
                        last = pe.matmul(xb[0][hh * S:(hh + 1) * S, b * 64:(b + 1) * 64],
                                         ctx_v[u][:, b * S:(b + 1) * S], wts[:, W_V + hh * 64:W_V + (hh + 1) * 64],
                                         start=True, stop=True)
                last.then_inc(v_mm, 1)

            def scores(i, u, p):
                g = nr(i, u)
                if p == 0:
                    pe.wait_ge(k_in[u], K_SPREAD * (i + 1))
                if p % HALF == 0:
                    pe.wait_ge(q_blocks, 2 * g + p // HALF + 1)
                for b in range(GB):
                    last = pe.matmul(sc[p % 2][:, b * S:(b + 1) * S], Qb[:, p, b, :, :],
                                     Kn[u][:, p, b * S:(b + 1) * S], start=True, stop=True)
                last.then_inc(s_mm, 1)

            def transpose_shift(i, u):
                pe.wait_ge(neg_done, nr(i, u) + 1)
                dst = xb[1][0:SHIFT_COLS, :].bitcast(BF16)
                for b in range(GB):
                    last = pe.transpose(dst[:, b * P:(b + 1) * P], neg_parts[:, b, :], identb[:, :])
                last.then_inc(shift_mm, 1)

            def scores_t(i, u, s):
                g = nr(i, u)
                if s == 0:
                    pe.wait_ge(k_blocks[0], g + 3)
                    pe.wait_ge(k_blocks[1], g + 1)
                    pe.wait_ge(shift_in, 16 * (g + 1))
                if s >= 2:
                    pe.wait_ge(exp_done, PAIRS * g + s - 1)
                p = ORDER[s]
                for b in range(GB):
                    cols = slice(b * S, (b + 1) * S)
                    last = pe.matmul(st[s % 2][:, cols], Ks[u][0:ROWS + SHIFT_ROWS, p, b, :, :],
                                     Qs[u][0:ROWS + SHIFT_ROWS, p, cols], start=True, stop=True)
                last.then_inc(st_mm, 1)

            def weigh(i, u, half, batches):
                g = nr(i, u)
                if batches[0] == 0:
                    pe.wait_ge(exp_done, PAIRS * g + HALF * (half + 1))
                    if half == 0:
                        pe.wait_ge(v_done, g + 1)
                for b in batches:
                    for s in range(half * HALF, (half + 1) * HALF):
                        p = ORDER[s]
                        j = p // 2
                        last = pe.matmul(o_ps[32 * j:32 * j + 32, b * S:(b + 1) * S], Vs[u][:, b, p, :],
                                  probs[:, p, b * S:(b + 1) * S], start=(half == 0 and b == 0),
                                  stop=(half == 1 and b == GB - 1), skip_group_check=True)
                if half == 1 and batches[-1] == GB - 1:
                    last.then_inc(o_mm, 1)

            def denominators(i, u, half):
                pe.wait_ge(exp_done, PAIRS * nr(i, u) + HALF * (half + 1))
                for s in range(half * HALF, (half + 1) * HALF):
                    p = ORDER[s]
                    j, q = p // 2, p % 2
                    last = pe.matmul(den_ps[32 * j:32 * j + 32, :], cst[:, C_ONES + 32 * q:C_ONES + 32 * q + 32],
                                     probs[:, p, :], start=(half == 0), stop=(half == 1), skip_group_check=True)
                    if s == 0:
                        last.then_inc(qs_used, 1)
                if half == 1:
                    last.then_inc(den_mm, 1)

            def mix(i, u, n):
                g = nr(i, u)
                pe.wait_ge(xt_biased, g + 1)
                pe.wait_ge(norm_done, 2 * g + n + 1)
                for t in (2 * n, 2 * n + 1):
                    dst = sc[t // 2][:, (t % 2) * DX:(t % 2 + 1) * DX]
                    pe.matmul(dst, attnT[:, t * P:(t + 1) * P], rhs_attn, start=True, stop=False)
                    last = pe.matmul(dst, xT[u][:, t * P:(t + 1) * P], rhs_x, start=False, stop=True)
                    if t % 2:
                        last.then_inc(mix_mm, 1)

            pe.wait_ge(w_in, 16)
            k_proj(0, 0)
            pe.wait_ge(c_in, 32)
            pe.matmul(st[0][:, 0:E], cst[:, C_CENTRE:C_CENTRE + P], wts[:, W_G:W_G + E],
                      start=True, stop=True).then_inc(setup_pe, 1)
            transpose_xn(0, 0)
            pe.wait_ge(setup_dve, 3)
            pe.matmul(st[1][:, 0:E], wts[:, W_ON:W_ON + D], cst[:, C_IDENT + P:C_IDENT + DX],
                      start=True, stop=True).then_inc(setup_pe, 1)
            pe.wait_ge(k_copied, 2)
            q_proj(0, 0)
            pe.wait_ge(setup_dve, 4)
            pe.transpose(st[0][:, P:2 * P], ident, ident).then_inc(qs_used, 1)
            pe.matmul(st[0][:, 0:1], wts[:, W_OT:W_OT + D], wts[:, W_BIAS + 2:W_BIAS + 3],
                      start=True, stop=True).then_inc(setup_pe, 1)
            transpose_xn(0, 1)
            pe.wait_ge(q_copied, 2)
            q_proj(0, 1)
            pe.wait_ge(q_copied, 4)
            k_proj(0, 1)
            for p in range(PAIRS):
                if p >= 2:
                    pe.wait_ge(max_done, p - 1)
                scores(0, 0, p)
                if p == 1:
                    pe.wait_ge(k_copied, 4)
                    k_proj(1, 0)
            pe.wait_ge(xnT_done, 2)
            pe.wait_ge(c_in, 32)
            transpose_shift(0, 0)
            pe.wait_ge(k_copied, 6)
            v_proj(0, 0)
            pe.wait_ge(shift_copied, 1)
            transpose_xn(1, 0)
            pe.wait_ge(ones_in[0], 16)
            pe.wait_ge(ones_in[1], 16)
            pe.wait_ge(setup_dve, 5)

            def step(i, u):
                g = nr(i, u)
                one, two, three = (after(i, u, n) for n in range(1, 4))
                near, far = range(GB // 2), range(GB // 2, GB)

                def next_scores(p):
                    if one is None:
                        return
                    if p == 0:
                        pe.wait_ge(x1_done, 2 * (g + 1))
                    elif p >= 2:
                        pe.wait_ge(max_done, PAIRS * (g + 1) + p - 1)
                    scores(*one, p)

                scores_t(i, u, 0)
                next_scores(0)
                scores_t(i, u, 1)
                next_scores(1)
                if two:
                    pe.wait_ge(v_done, g + 1)
                    pe.wait_ge(k_copied, 2 * (g + 3))
                    q_proj(*two)
                next_scores(2)
                scores_t(i, u, 2)
                next_scores(3)
                scores_t(i, u, 3)
                next_scores(4)
                next_scores(5)
                scores_t(i, u, 4)
                next_scores(6)
                if one:
                    weigh(i, u, 0, range(0, 1))
                scores_t(i, u, 5)
                next_scores(7)
                if one:
                    weigh(i, u, 0, range(1, 2))
                    scores_t(i, u, 6)
                    scores_t(i, u, 7)
                    denominators(i, u, 0)
                else:
                    denominators(i, u, 0)
                    scores_t(i, u, 6)
                    weigh(i, u, 0, near)
                    scores_t(i, u, 7)
                    weigh(i, u, 0, far)
                if one:
                    if two:
                        pe.wait_ge(xnT_done, g + 3)
                    transpose_shift(*one)
                denominators(i, u, 1)
                if three:
                    pe.wait_ge(q_copied, 2 * (g + 3))
                    k_proj(*three)
                if one:
                    weigh(i, u, 0, range(2, GB))
                weigh(i, u, 1, range(GB))
                if one:
                    if three:
                        pe.wait_ge(k_copied, 2 * (g + 4))
                    elif two:
                        pe.wait_ge(q_copied, 2 * (g + 3))
                    v_proj(*one)
                    pe.wait_ge(max_done, PAIRS * (g + 2))
                mix(i, u, 0)
                mix(i, u, 1)
                if three:
                    pe.wait_ge(shift_copied, g + 2)
                    transpose_xn(*three)

            with pe.Fori(0, LOOPS) as i:
                step(i, 0)
                step(i, 1)
            for g in range(2 * LOOPS, G):
                step(g // 2, g % 2)
            pe.wait_ge(gates_done, 2)
            pe.matmul(st[0][:, 0:G * NT * E], onesb[:, :], picked[:, :], start=True, stop=True).then_inc(count_mm, 1)
            pe.wait_ge(keep_known, 1)
            go = pe.value_load(any_keep_i[0:1, 0:1], min_val=0, max_val=1)
            with pe.If(go > 0):
                pe.wait_ge(ew_in, 64)
                with pe.Fori(0, G) as g:
                    pe.wait_ge(xe_done, g + 1)
                    for t in range(NT):
                        ins = pe.transpose(xb[1][:, t * P:(t + 1) * P], xe_n[:, t, :], ident)
                    ins.then_inc(xeT_mm, 1)
                    pe.wait_ge(xeT_done, g + 1)

                    def hid(e):
                        if e:
                            pe.wait_ge(hid_done, E * g + e)
                        pe.matmul(xb[0][:, :], w1s[:, e, :], xeT[:, :], start=True, stop=True).then_inc(hid_mm, 1)

                    hid(0)
                    for e in range(E):
                        pe.wait_ge(hid_done, E * g + e + 1)
                        if e + 1 < E:
                            hid(e + 1)
                        if e >= 2:
                            pe.wait_ge(y_added, NT * E * g + NT * (e - 1))
                        for t in range(NT):
                            dst = st[e % 2][:, t * D:(t + 1) * D]
                            pe.matmul(dst, hidden[e % 2][:, t * P:(t + 1) * P], w2s[:, e, :], start=True, stop=False)
                            ins = pe.matmul(dst, one_row[:, :], b2s[:, e, :], start=False, stop=True)
                        ins.then_inc(y_mm, 1)


def kernel(**inputs):
    import ml_dtypes
    import numpy as np
    import concourse.bacc as bacc
    from concourse.bass_utils import run_bass_kernel_spmd

    a = {k: np.asarray(v) for k, v in inputs.items()}
    x = np.ascontiguousarray(a["x"].reshape(TOK, D))
    ctx = a["ctx_1024"].reshape(TOK, D)

    def by_group(m):
        return np.ascontiguousarray(m.reshape(G, GT, D).transpose(0, 2, 1))

    w = np.zeros((D, W_COLS), np.float32)
    order = np.arange(D).reshape(PAIRS, 2 * DK).T.reshape(D)
    w[:, W_Q:W_Q + D] = a["L0_xattn_Wq"].T[:, order]
    w[:, W_K:W_K + D] = a["L0_xattn_Wk"].T[:, order]
    w[:, W_V:W_V + D] = a["L0_xattn_Wv"].reshape(PAIRS, 2, DK, D).transpose(3, 1, 0, 2).reshape(D, D)
    w[:, W_OT:W_OT + D] = a["L0_xattn_Wo"].T
    w[:, W_ON:W_ON + D] = a["L0_xattn_Wo"]
    w[:, W_G:W_G + E] = a["L0_ffn_gate_w"].T
    for n, name in enumerate(("bq", "bk", "bv", "bo")):
        w[:, W_BIAS + n] = a["L0_xattn_" + name][order] if name in ("bq", "bk") else a["L0_xattn_" + name]
    c = np.zeros((P, C_COLS), np.float32)
    c[:, C_IDENT:C_IDENT + P] = np.eye(P)
    c[:, C_CENTRE:C_CENTRE + P] = np.eye(P) - 1.0 / D
    for q in range(2):
        for hh in range(2):
            first = C_ONES + 32 * q + 16 * q + 8 * hh
            c[hh * S:(hh + 1) * S, first:first + DK] = 1.0
    c[:, C_DESC:C_DESC + E] = np.arange(E, 0, -1)
    for hh in range(2):
        c[:ROWS, C_MASK + hh] = np.arange(ROWS) // DK % 2 == hh
    ones = np.zeros((SHIFT_ROWS, PAIRS, GB, 2, S), ml_dtypes.bfloat16)
    for hh in range(2):
        ones[hh * PARTS:(hh + 1) * PARTS, :, :, hh] = 1.0
    arrays = {
        "x_nat": x, "x_t": by_group(x), "ctx_t": by_group(ctx), "weights": w, "consts": c, "shift_ones": ones,
        "ident_b": np.eye(P).astype(ml_dtypes.bfloat16),
        "w1": np.ascontiguousarray(a["L0_ffn_W1"].transpose(1, 0, 2)),
        "w2": np.ascontiguousarray(a["L0_ffn_W2"].transpose(1, 0, 2)),
        "b1_t": np.ascontiguousarray(a["L0_ffn_b1"].T),
        "b2_rows": np.ascontiguousarray(a["L0_ffn_b2"].reshape(1, E, D)),
    }
    nc = bacc.Bacc("TRN2", target_bir_lowering=False, num_devices=1)
    aps = [nc.dram_tensor(n, v.shape, mybir.dt.from_np(v.dtype), kind="ExternalInput").ap()
           for n, v in arrays.items()]
    out = nc.dram_tensor("out", (TOK, D), F32, kind="ExternalOutput").ap()
    build(nc, *aps, out)
    r = run_bass_kernel_spmd(nc, [arrays], core_ids=[0])
    return r.results[0]["out"].reshape(B, S, D)
```
